# Optimizing a Trainium2 kernel written in Bass

```python
import numpy as np
import jax
import jax.numpy as jnp

def _softmax(x, axis=-1):
    return jax.nn.softmax(x, axis=axis)

def _gelu(x):
    return jax.nn.gelu(x, approximate=True)

def _silu(x):
    return jax.nn.silu(x)

def _sigmoid(x):
    return jax.nn.sigmoid(x)

def _layernorm(x, axis=-1, eps=1e-05):
    m = jnp.mean(x, axis=axis, keepdims=True)
    v = jnp.var(x, axis=axis, keepdims=True)
    return (x - m) / jnp.sqrt(v + eps)

def _scatter_add(tgt, idx, src, axis=0):
    return tgt.at[idx].add(src)

def _segment_sum(src, seg, n):
    return jax.ops.segment_sum(src, seg, n)
kernel_name = 'mk_cond_resid_d2_seqx_r4_3362b5'

def setup_inputs(seed: int=0):
    np.random.seed(seed)
    _w = jnp.asarray

    def _rec_inputs():
        import jax
        import jax.numpy as jnp
        _rk = jax.random.key(seed)
        x = -0.0003929 + 0.9999 * jax.random.normal(jax.random.fold_in(_rk, 1), (32, 64, 1024), jnp.float32)
        _lenS = 64 - jax.random.randint(jax.random.fold_in(_rk, 7), (32,), 0, max(1, 64 // 4) + 1, jnp.int32)
        _lenS2 = 64 - jax.random.randint(jax.random.fold_in(_rk, 8), (32,), 0, max(1, 64 // 4) + 1, jnp.int32)
        itok_B_8_3872 = jax.random.randint(jax.random.fold_in(_rk, 11), (32,), 8, 3873, jnp.int32)
        itok_B_3_7 = jax.random.randint(jax.random.fold_in(_rk, 12), (32,), 3, 8, jnp.int32)
        return (x, itok_B_8_3872, itok_B_3_7)
    x, itok_B_8_3872, itok_B_3_7 = _rec_inputs()

    def _L0_cond_setup():
        import math
        import jax, jax.numpy as jnp
        import numpy as np
        H, N, B, L = (64, 64, 16, 1024)
        DT_MIN, DT_MAX = (0.001, 0.1)

        def _get_kernel(log_dt, C, log_A_real, A_imag, length):
            Cc = C[..., 0] + 1j * C[..., 1]
            dt = jnp.exp(log_dt)
            A = -jnp.exp(log_A_real) + 1j * A_imag
            dtA = A * dt[:, None]
            P = dtA[:, :, None] * jnp.arange(length, dtype=jnp.float32)
            Cs = Cc * (jnp.exp(dtA) - 1.0) / A
            K = 2.0 * jnp.einsum('hn,hnl->hl', Cs, jnp.exp(P)).real
            return K
        key = jax.random.key(seed)
        ks = jax.random.split(key, 6)
        u = jax.random.normal(ks[0], (B, H, L), dtype=jnp.float32)
        length = jax.random.randint(ks[1], (B,), 0, L)
        log_dt = jax.random.uniform(ks[2], (H,), dtype=jnp.float32) * (math.log(DT_MAX) - math.log(DT_MIN)) + math.log(DT_MIN)
        C = jax.random.normal(ks[3], (H, N, 2), dtype=jnp.float32)
        log_A_real = jnp.log(0.5 * jnp.ones((H, N), dtype=jnp.float32))
        A_imag = math.pi * jnp.broadcast_to(jnp.arange(N, dtype=jnp.float32), (H, N))
        D = jax.random.normal(ks[4], (H,), dtype=jnp.float32)
        return {'u': u, 'length': length, 'log_dt': log_dt, 'C': C, 'log_A_real': log_A_real, 'A_imag': A_imag, 'D': D}
    _L0_cond_all = _L0_cond_setup()
    _L0_cond_in = {k: v for k, v in _L0_cond_all.items() if k in ('log_dt', 'C', 'log_A_real', 'A_imag', 'D')}
    del _L0_cond_all

    def _L1_cond_setup():
        import jax, jax.numpy as jnp
        import numpy as np
        MAX_LORAS, OUT, IN = (8, 1024, 1024)
        B, S = (4, 512)
        key = jax.random.key(seed)
        k1, k2, k3 = jax.random.split(key, 3)
        x = jax.random.normal(k1, (B, S, IN), dtype=jnp.float32)
        weight = jax.random.normal(k2, (MAX_LORAS, OUT, IN), dtype=jnp.float32) * 0.02
        adapter_ids = jax.random.randint(k3, (B,), 0, MAX_LORAS, dtype=jnp.int32)
        return {'x': x, 'weight': weight, 'adapter_ids': adapter_ids}
    _L1_cond_all = _L1_cond_setup()
    _L1_cond_in = {k: v for k, v in _L1_cond_all.items() if k in ('weight',)}
    del _L1_cond_all
    return {'x': x, 'itok_B_8_3872': itok_B_8_3872, 'itok_B_3_7': itok_B_3_7, 'L0_cond_log_dt': _L0_cond_in['log_dt'], 'L0_cond_C': _L0_cond_in['C'], 'L0_cond_log_A_real': _L0_cond_in['log_A_real'], 'L0_cond_A_imag': _L0_cond_in['A_imag'], 'L0_cond_D': _L0_cond_in['D'], 'L1_cond_weight': _L1_cond_in['weight']}

def reference(x, itok_B_8_3872, itok_B_3_7, L0_cond_log_dt, L0_cond_C, L0_cond_log_A_real, L0_cond_A_imag, L0_cond_D, L1_cond_weight):
    import jax
    import jax.numpy as jnp

    def _L0_cond_ref(u, length, log_dt, C, log_A_real, A_imag, D):
        import math
        import jax, jax.numpy as jnp
        import numpy as np
        H, N, B, L = (64, 64, 16, 1024)
        DT_MIN, DT_MAX = (0.001, 0.1)

        def _get_kernel(log_dt, C, log_A_real, A_imag, length):
            Cc = C[..., 0] + 1j * C[..., 1]
            dt = jnp.exp(log_dt)
            A = -jnp.exp(log_A_real) + 1j * A_imag
            dtA = A * dt[:, None]
            P = dtA[:, :, None] * jnp.arange(length, dtype=jnp.float32)
            Cs = Cc * (jnp.exp(dtA) - 1.0) / A
            K = 2.0 * jnp.einsum('hn,hnl->hl', Cs, jnp.exp(P)).real
            return K
        Bq, Hq, Lq = u.shape
        mask = (jnp.arange(Lq) < length[:, None]).astype(u.dtype)
        u_m = u * mask[:, None, :]
        kernel = _get_kernel(log_dt, C, log_A_real, A_imag, Lq)
        n = 2 * Lq
        k_f = jnp.fft.rfft(kernel, n=n)
        u_f = jnp.fft.rfft(u_m, n=n)
        y = jnp.fft.irfft(u_f * k_f, n=n)[..., :Lq]
        y = y + u_m * D[:, None]
        return y * mask[:, None, :]

    def _L1_cond_ref(x, weight, adapter_ids):
        import jax, jax.numpy as jnp
        import numpy as np
        MAX_LORAS, OUT, IN = (8, 1024, 1024)
        B, S = (4, 512)
        w = weight[adapter_ids]
        return jnp.einsum('bsi,boi->bso', x, w)
    x = x + _L0_cond_ref(x, itok_B_8_3872, L0_cond_log_dt, L0_cond_C, L0_cond_log_A_real, L0_cond_A_imag, L0_cond_D)
    x = x + _L1_cond_ref(x, L1_cond_weight, itok_B_3_7)
    return x

_drawn_inputs = setup_inputs


def setup_inputs(seed=0):
    import zlib

    import numpy as np

    out = dict(_drawn_inputs(seed))
    spreads = {'L0_cond_log_A_real': (-0.6931471824645996, 0.2)}
    factors = {}
    for name, (base, spread) in spreads.items():
        noise = np.random.default_rng([zlib.crc32(name.encode()), seed]).standard_normal(out[name].shape)
        drawn = base * np.exp(spread * noise) if base else spread * noise
        out[name] = jnp.asarray(drawn.astype(out[name].dtype))
    for name, factor in factors.items():
        out[name] = (out[name] * factor).astype(out[name].dtype)
    return out
```

```python
import math
from contextlib import ExitStack

import concourse.bass as bass
from concourse import mybir


class Chain:

    def __init__(self, engine, semaphore):
        self.engine, self.semaphore, self.base, self.n = engine, semaphore, 0, 0

    def turn(self, base):
        self.base, self.n = base, 0

    def link(self, instruction):
        self.n += 1
        instruction.then_inc(self.semaphore, 1)
        self.engine.wait_ge(self.semaphore, self.base + self.n)


def ssm_conv_then_adapter_kernel(nc, x_in, x_rev_in, ids_in, lens_in, log_dt_in, log_a_in, a_imag_in, c_in, d_in, w_in, out):
    f32, f32r, i32 = mybir.dt.float32, mybir.dt.float32r, mybir.dt.int32
    ALU = mybir.AluOpType
    ACT = mybir.ActivationFunctionType
    AX = mybir.AxisListType.X

    P = 128
    B, H, L = out.shape
    N = a_imag_in.shape[0]
    NA = w_in.shape[0]
    NB = L // P
    COL = NB * B
    GH = 8
    NG = H // GH
    NPAIR = GH // 2
    S = 32
    KROW = L + P
    Q = 4
    CQ = NB // Q
    SLOTS = (B + NA) // 2
    SURE = B // 2
    POS = 2 * (SLOTS + 1)
    FIELDS = 8
    F_B0, F_B1, F_FIRST, F_ADAPTER, F_TWO, F_ACTIVE, F_NUMBER, F_ODD = range(FIELDS)
    PEEL = 4
    HALF = L // 2

    INV_2PI = 1.0 / (2.0 * math.pi)
    TWO_PI_HI = 6.28125
    TWO_PI_LO = 2.0 * math.pi - TWO_PI_HI
    PI_BELOW = 3.141592
    LOG2E = 1.0 / math.log(2.0)
    LN2_HI = 0.693359375
    LN2_LO = math.log(2.0) - LN2_HI

    ctx = ExitStack()
    with ctx:
        def sem(name):
            return ctx.enter_context(nc.semaphore(name))

        def tile(where, name, shape, dt=f32):
            return where.enter_context(nc.sbuf_tensor(name, shape, dt))

        z = tile(ctx, "z", [P, H, COL])
        z_group = z[:, :, :].rearrange("p (g h) n -> p g (h n)", g=NG)
        z_pair = z[:, :, :].rearrange("p (k e) n -> p k e n", e=2)
        z_hcb = z[:, :, :].rearrange("p h (c b) -> p c h b", c=NB)
        mask = tile(ctx, "mask", [P, NB, B])
        ident = tile(ctx, "ident", [P, P])
        table = tile(ctx, "table", [1, (SLOTS + 1) * FIELDS], i32)
        w_hi = tile(ctx, "w_hi", [P, NB, L], f32r)
        with ExitStack() as early:
            tile(early, "lower_quarters_of_w_lo", [P, NB // 2, L])
            x_rev = tile(early, "x_rev", [P, 2, GH * COL])
        w_lo = tile(ctx, "w_lo", [P, NB, L], f32r)

        with ExitStack() as early:
            mag = tile(early, "mag", [P, 2, H, S])
            phase = tile(early, "phase", [P, 2, GH, S])
            turns = tile(early, "turns", [P, 2, GH, S], i32)
            sine = tile(early, "sine", [P, 2, GH, S])
            factor = tile(early, "factor", [P, 2, GH, S])
            swapped = tile(early, "swapped", [P, GH, S])
            left = tile(early, "left", [P, GH, S])
            k_tile = tile(early, "k_tile", [S, GH, S])
            k_skip = tile(early, "k_skip", [S, GH, S])
            ctl = tile(early, "ctl", [B, 1024])
        w_raw = tile(ctx, "w_raw", [P, NB, L])
        w_diag = w_raw[:, :, :].rearrange("p c n -> p (c n)")

        with ExitStack() as early:
            strips = tile(early, "strips", [P, NPAIR, 2, L])
            mid = tile(early, "mid", [P, 2, 2, COL])
            small = tile(early, "small", [P, 36 * H])
        z_hi = tile(ctx, "z_hi", [P, 2, NB, P], f32r)
        z_lo = tile(ctx, "z_lo", [P, 2, NB, P], f32r)
        o_tile = tile(ctx, "o_tile", [P, 2, L])

        taken = [0]

        def small_tile(n, dt=f32, parts=P):
            v = small[0:parts, taken[0]:taken[0] + n]
            taken[0] += n
            assert taken[0] <= 36 * H
            return v if dt == f32 else v.bitcast(dt)

        exponent = small_tile(2 * H)
        kint = small_tile(2 * H, i32)
        rest = small_tile(2 * H)
        expm = small_tile(2 * H)
        scale2 = small_tile(2 * H, i32)
        scale2f = scale2.bitcast(f32)
        expd = small_tile(2 * H)
        dt_, ea = expd[:, 0:H], expd[:, H:2 * H]
        a_im = small_tile(H)
        c_ri = small_tile(2 * H)
        c_re, c_im = c_ri[:, 0:H], c_ri[:, H:2 * H]
        dre = small_tile(H)
        ang2 = small_tile(2 * H)
        dim = ang2[:, 0:H]
        phase_dim = small_tile(H)
        sin2 = small_tile(2 * H)
        e_re = small_tile(H)
        e_im = small_tile(H)
        n_re = small_tile(H)
        n_im = small_tile(H)
        tmp_a = small_tile(H)
        tmp_b = small_tile(H)
        alpha = small_tile(H)
        beta = small_tile(H)
        d_row = small_tile(H, parts=S)
        power = small_tile(2 * S)
        cols = small_tile(5)
        quarter, halfpi, sign, lowest, highest = (cols[:, i:i + 1] for i in range(5))
        corner = small_tile(S, parts=S)
        t_iota = small_tile(NB)
        lens_i = small_tile(B, i32)
        lens = small_tile(B)

        at = [0]

        def ctl_tile(n, dt=f32):
            v = ctl[:, at[0]:at[0] + n]
            at[0] += n
            assert at[0] <= 1024
            return v if dt == f32 else v.bitcast(dt)

        ids_i = ctl_tile(B + 1, i32)
        ids = ctl_tile(B + 1)
        wrap = ctl_tile(B + 1)
        own = ids[:, B:B + 1]
        below = ctl_tile(B)
        same = ctl_tile(B)
        rank = ctl_tile(1)
        iota_a = ctl_tile(NA)
        is_a = ctl_tile(NA * B)
        count = ctl_tile(NA)
        pairs_i = ctl_tile(NA, i32)
        less = ctl_tile(NA)
        before = ctl_tile(1)
        pos = ctl_tile(1)
        iota_pos = ctl_tile(POS)
        match = ctl_tile(POS)
        values = ctl_tile(3)
        row = ctl_tile(7 * POS)[0:1, :].rearrange("p (f n) -> p f n", f=7)

        banks = [ctx.enter_context(nc.psum_tensor(f"bank{i}", [P, 512], f32)) for i in range(6)]
        conv_ps = banks[0:NPAIR]
        k_ps = banks[4]
        table_ps = banks[5]
        slot_ps = [[banks[0], banks[1]], [banks[2], banks[3]]]

        k_dram = nc.dram_tensor("k_padded", [H, KROW], f32, kind="Internal")
        k_strips = bass.AP(tensor=k_dram, offset=1, ap=[[2 * KROW, H // 2], [1, P], [KROW, 2], [1, L]])
        k_rows = k_dram[:, P:KROW].rearrange("(g h) (a b) -> g a h b", g=NG, a=S)

        params_in = sem("params_in")
        control_in = sem("control_in")
        x_in_sem, x_rev_in_sem = sem("x_loaded"), sem("x_rev_loaded")
        consts = sem("consts")
        dve_step, pool_step = sem("dve_step"), sem("pool_step")
        dre_ready = sem("dre_ready")
        e_ready = sem("e_ready")
        mag_ready = sem("mag_ready")
        angles2 = sem("angles2")
        sin2_ready = sem("sin2_ready")
        coef_ready = sem("coef_ready")
        ctl_ready, slots_placed = sem("ctl_ready"), sem("slots_placed")
        table_rows, table_ready = sem("table_rows"), sem("table_ready")
        angle_step = sem("angle_step")
        angle_ready, sine_ready = sem("angle_ready"), sem("sine_ready")
        factor_ready, swap_ready = sem("factor_ready"), sem("swap_ready")
        left_ready = sem("left_ready")
        skip_ready = sem("skip_ready")
        k_made, k_out = sem("k_made"), sem("k_out")
        k_stored = sem("k_stored")
        zeros_ready, zeros_stored = sem("zeros_ready"), sem("zeros_stored")
        strip_in = [sem(f"strip_in{k}") for k in range(NPAIR)]
        conv_done = sem("conv_done")
        masked = sem("masked")
        added = sem("added")
        raw_in = [sem(f"raw_in{q}") for q in range(Q)]
        diag_ready = sem("diag_ready")
        w_hi_ready, w_lo_ready = sem("w_hi_ready"), sem("w_lo_ready")
        w_used = sem("w_used")
        z_hi_ready, z_lo_ready = sem("z_hi_ready"), sem("z_lo_ready")
        out_act, out_dve = sem("out_act"), sem("out_dve")
        stored = [sem("stored0"), sem("stored1")]
        all_stored = sem("all_stored")

        NCONST = 16

        block = ctx.enter_context(nc.Block())

        def field(engine, s, f, top):
            return engine.value_load(table[0:1, bass.ds(s * FIELDS + f, 1)], min_val=0, max_val=top)

        def slot_loop(engine, body):
            for s in range(1, PEEL):
                body(s, s % 2, s // 2)
            with engine.Fori(PEEL // 2, SURE // 2) as t:
                for par in range(2):
                    body(2 * t + par, par, t)
            with engine.Fori(SURE // 2, SLOTS // 2) as t:
                for par in range(2):
                    active = field(engine, 2 * t + par, F_ACTIVE, 1)
                    with engine.If(active == 1):
                        body(2 * t + par, par, t)

        def last_slot(engine, body):
            but_two = engine.value_load(table[0:1, SLOTS * FIELDS + F_NUMBER:SLOTS * FIELDS + F_NUMBER + 1],
                                  min_val=SURE - 2, max_val=SLOTS - 2)
            odd = field(engine, SLOTS, F_ODD, 1)
            with engine.If(odd == 1):
                body(but_two, 0)
            with engine.Else():
                body(but_two, 1)

        @block.sync
        def _(sp):
            both = lambda ap: [(0, ap), (N, ap)]
            for lo, src in both(a_imag_in):
                sp.dma_start(a_im[lo:lo + N, :], src).then_inc(params_in, 16)
            for lo, src in both(log_a_in):
                sp.dma_start(exponent[lo:lo + N, H:2 * H], src).then_inc(params_in, 16)
            sp.dma_start(exponent[:, 0:H], log_dt_in.to_broadcast([P, H])).then_inc(params_in, 16)
            for e in range(2):
                for lo, src in both(c_in[e]):
                    sp.dma_start(c_ri[lo:lo + N, e * H:(e + 1) * H], src).then_inc(params_in, 16)
            sp.dma_start(d_row, d_in.to_broadcast([S, H])).then_inc(params_in, 16)
            sp.dma_start(lens_i, lens_in.to_broadcast([P, B])).then_inc(control_in, 16)
            sp.dma_start(ids_i[:, 0:B], ids_in.to_broadcast([B, B])).then_inc(control_in, 16)
            with nc.allow_non_contiguous_dma(reason="one id per partition"):
                sp.dma_start(ids_i[:, B:B + 1], ids_in.rearrange("a b -> b a")).then_inc(control_in, 16)

            def load_x(g):
                if not (isinstance(g, int) and g == 0):
                    sp.wait_ge(x_rev_in_sem, 16 * g)
                    sp.wait_ge(x_in_sem, 16 * g)
                if not (isinstance(g, int) and g < 2):
                    sp.wait_ge(conv_done, (g - 1) * NPAIR)
                sp.dma_start(x_rev[:, bass.ds(g % 2, 1), :].rearrange("p o n -> p (o n)"),
                             x_rev_in[bass.ds(g, 1)].rearrange("o p n -> (o p) n")).then_inc(x_rev_in_sem, 16)
                sp.dma_start(z_group[:, bass.ds(g, 1), :].rearrange("p o n -> p (o n)"),
                             x_in[bass.ds(g, 1)].rearrange("o p n -> (o p) n")).then_inc(x_in_sem, 16)

            load_x(0)
            load_x(1)
            def load_strips(g):
                sp.wait_ge(k_stored, 16 * (g + 1))
                for k in range(NPAIR):
                    if not (isinstance(g, int) and g == 0):
                        sp.wait_ge(conv_done, (g - 1) * NPAIR + k + 1)
                    sp.dma_start(strips[:, k, :, :],
                                 k_strips[bass.ds(g * NPAIR + k, 1)].rearrange("o j e m -> (o j) e m")
                                 ).then_inc(strip_in[k], 16)

            def load_weights(s, adapter):
                for q in range(Q):
                    if isinstance(s, int) and s == 0:
                        pass
                    else:
                        sp.wait_ge(w_lo_ready, Q * (s - 1) + q + 1)
                    sp.dma_start(w_raw[:, CQ * q:CQ * (q + 1), :].rearrange("p c n -> p (c n)"),
                                 w_in[bass.ds(adapter, 1), q].rearrange("o p n -> (o p) n")
                                 ).then_inc(raw_in[q], 16)

            sp.wait_ge(zeros_stored, 16)
            load_strips(0)
            with sp.Fori(1, NG - 1) as g:
                load_strips(g)
                load_x(g + 1)
            sp.wait_ge(k_stored, 16 * NG)
            sp.wait_ge(table_ready, 1)
            load_weights(0, field(sp, 0, F_ADAPTER, NA - 1))
            load_strips(NG - 1)

            def weights_ahead(s):
                first = field(sp, s, F_FIRST, 1)
                adapter = field(sp, s, F_ADAPTER, NA - 1)
                with sp.If(first == 1):
                    load_weights(s, adapter)
                with sp.Else():
                    for q in range(Q):
                        sp.wait_ge(raw_in[q], 16 * s)
                        sp.sem_inc(raw_in[q], 16)

            def store_slot(s, par):
                b0 = field(sp, s, F_B0, B - 1)
                b1 = field(sp, s, F_B1, B - 1)
                two = field(sp, s, F_TWO, 1)
                sp.wait_ge(out_act, s + 1)
                sp.wait_ge(out_dve, s + 1)
                sp.dma_start(out[bass.ds(b0, 1)].rearrange("o h n -> (o h) n"),
                             o_tile[0:H, par, :]).then_inc(stored[par], 16)
                sp.dma_start(out[bass.ds(b1, 1)].rearrange("o h n -> (o h) n"),
                             o_tile[H:P, par, :], cond=two == 1).then_inc(stored[par], 16)

            def slot(s, par, t):
                weights_ahead(s + 1)
                store_slot(s - 1, 1 - par)

            def finish_last(m, par):
                store_slot(m + 1, par)
                for parity, value in ((par, 16 * (m + 3 - par)), (1 - par, 16 * (m + 1 + par))):
                    sp.wait_ge(stored[parity], value)
                    sp.sem_inc(all_stored, 1)

            weights_ahead(1)
            slot_loop(sp, slot)
            last_slot(sp, finish_last)
            sp.wait_ge(all_stored, 2)

        @block.gpsimd
        def _(pool):
            chain = Chain(pool, pool_step)
            constant = Chain(pool, consts)
            constant.link(nc.gpsimd.memset(quarter[0:N, :], 0.25))
            constant.link(nc.gpsimd.memset(quarter[N:P, :], 0.0))
            constant.link(nc.gpsimd.memset(halfpi[0:N, :], math.pi / 2))
            constant.link(nc.gpsimd.memset(halfpi[N:P, :], 0.0))
            constant.link(nc.gpsimd.memset(sign[0:N, :], 2.0))
            constant.link(nc.gpsimd.memset(lowest[0:N, :], -PI_BELOW - math.pi / 2))
            constant.link(nc.gpsimd.memset(lowest[N:P, :], -PI_BELOW))
            constant.link(nc.gpsimd.memset(highest[0:N, :], PI_BELOW - math.pi / 2))
            constant.link(nc.gpsimd.memset(highest[N:P, :], PI_BELOW))
            constant.link(nc.gpsimd.memset(sign[N:P, :], -2.0))
            exact = dict(allow_small_or_imprecise_dtypes=True)
            constant.link(nc.gpsimd.iota(power[:, 0:S], [[S, S]], base=0, channel_multiplier=0, **exact))
            constant.link(nc.gpsimd.iota(power[:, S:2 * S], [[1, S]], base=0, channel_multiplier=0, **exact))
            constant.link(nc.gpsimd.iota(t_iota, [[P, NB]], base=0, channel_multiplier=1, **exact))
            constant.link(nc.gpsimd.iota(iota_a, [[1, NA]], base=0, channel_multiplier=0, **exact))
            constant.link(nc.gpsimd.iota(iota_pos, [[1, POS]], base=0, channel_multiplier=0, **exact))
            constant.link(nc.gpsimd.iota(values[:, 1:2], [[1, 1]], base=0, channel_multiplier=1, **exact))
            chain.link(nc.gpsimd.memset(corner, 1.0))
            chain.link(nc.gpsimd.affine_select(out=corner, in_=corner, compare_op=ALU.is_equal, fill=0.0,
                                               base=0, pattern=[[1, S]], channel_multiplier=S))
            chain.link(nc.gpsimd.memset(below, 1.0))
            chain.link(nc.gpsimd.affine_select(out=below, in_=below, compare_op=ALU.is_gt, fill=0.0,
                                               base=0, pattern=[[-1, B]], channel_multiplier=1))
            chain.link(nc.gpsimd.memset(ident[:, :], 1.0))
            chain.link(nc.gpsimd.affine_select(out=ident[:, :], in_=ident[:, :], compare_op=ALU.is_equal, fill=0.0,
                                               base=0, pattern=[[-1, P]], channel_multiplier=1))
            constant.link(nc.gpsimd.memset(values[:, 0:1], 1.0))
            pool.wait_ge(dre_ready, 1)
            for e in range(2):
                nc.gpsimd.tensor_tensor(mag[:, e, :, :], dre.unsqueeze(2).to_broadcast([P, H, S]),
                                        power[:, e * S:(e + 1) * S].unsqueeze(1).to_broadcast([P, H, S]),
                                        ALU.mult).then_inc(e_ready, 1)
            pool.wait_ge(params_in, 16 * 10)
            pool.wait_ge(coef_ready, 1)

            base = chain.n
            PER = 2

            def left_factor(g):
                chain.turn(base + PER * g)
                pool.wait_ge(factor_ready, g + 1)
                if not (isinstance(g, int) and g == 0):
                    pool.wait_ge(k_made, g)
                chain.link(nc.gpsimd.tensor_tensor(left[:, :, :], factor[:, 0, :, :],
                                                   alpha[:, bass.ds(g * GH, GH)].unsqueeze(2).to_broadcast([P, GH, S]),
                                                   ALU.mult))
                pool.wait_ge(swap_ready, 2 * (g + 1))
                chain.link(nc.gpsimd.tensor_tensor(swapped[:, :, :], swapped[:, :, :],
                                                   beta[:, bass.ds(g * GH, GH)].unsqueeze(2).to_broadcast([P, GH, S]),
                                                   ALU.mult))
                nc.gpsimd.tensor_tensor(left[:, :, :], left[:, :, :], swapped[:, :, :], ALU.add).then_inc(left_ready, 1)
                if not (isinstance(g, int) and g == 0):
                    pool.wait_ge(k_out, g)
                nc.gpsimd.tensor_tensor(k_skip[:, :, :], d_row[:, bass.ds(g * GH, GH)].unsqueeze(2).to_broadcast([S, GH, S]),
                                        corner.unsqueeze(1).to_broadcast([S, GH, S]), ALU.mult).then_inc(skip_ready, 1)

            def add_masked(g):
                pool.wait_ge(x_in_sem, 16 * (g + 1))
                for k in range(NPAIR):
                    n = g * NPAIR + k
                    pool.wait_ge(masked, n + 1)
                    nc.gpsimd.tensor_tensor(z_pair[:, bass.ds(n, 1)].rearrange("p o e n -> p (o e n)"),
                                            z_pair[:, bass.ds(n, 1)].rearrange("p o e n -> p (o e n)"),
                                            mid[:, k % 2, :, :].rearrange("p e n -> p (e n)"), ALU.add).then_inc(added, 1)

            left_factor(0)
            left_factor(1)
            with pool.Fori(0, NG - 2) as g:
                left_factor(g + 2)
                add_masked(g)
            add_masked(NG - 2)

            def add_identity(s):
                for q in range(Q):
                    pool.wait_ge(raw_in[q], 16 * (s + 1))
                    for c in range(CQ * q, CQ * (q + 1)):
                        nc.gpsimd.tensor_tensor(w_raw[:, c, c * P:(c + 1) * P], w_raw[:, c, c * P:(c + 1) * P],
                                                ident[:, :], ALU.add).then_inc(diag_ready, 1)

            add_identity(0)
            add_masked(NG - 1)

            def slot(s):
                first = field(pool, s, F_FIRST, 1)
                with pool.If(first == 1):
                    add_identity(s)
                with pool.Else():
                    pool.wait_ge(diag_ready, NB * s)
                    pool.sem_inc(diag_ready, NB)

            pool.wait_ge(table_ready, 1)
            with pool.Fori(1, SLOTS) as s:
                slot(s)

        @block.scalar
        def _(act):
            for e in range(2):
                act.wait_ge(e_ready, e + 1)
                nc.scalar.activation(mag[:, e, :, :].rearrange("p h s -> p (h s)"),
                                     mag[:, e, :, :].rearrange("p h s -> p (h s)"), ACT.Exp).then_inc(mag_ready, 1)
            act.wait_ge(angles2, 1)
            nc.scalar.activation(sin2, rest, ACT.Sin).then_inc(sin2_ready, 1)

            def trig(g):
                act.wait_ge(angle_ready, g + 1)
                if not (isinstance(g, int) and g == 0):
                    act.wait_ge(factor_ready, g)
                nc.scalar.activation(sine[:, :, :, :].rearrange("p e h s -> p (e h s)"),
                                     phase[:, :, :, :].rearrange("p e h s -> p (e h s)"),
                                     ACT.Sin, bias=halfpi).then_inc(sine_ready, 1)
                act.wait_ge(factor_ready, g + 1)
                if not (isinstance(g, int) and g == 0):
                    act.wait_ge(left_ready, g)
                nc.scalar.copy(swapped[0:N, :, :], factor[N:P, 0, :, :]).then_inc(swap_ready, 1)
                nc.scalar.copy(swapped[N:P, :, :], factor[0:N, 0, :, :]).then_inc(swap_ready, 1)
                act.wait_ge(k_out, g + 1)
                act.dma_start(k_rows[g] if isinstance(g, int) else k_rows[bass.ds(g, 1)].rearrange("o a h b -> (o a) h b"),
                              k_tile[:, :, :]).then_inc(k_stored, 16)

            act.wait_ge(zeros_ready, 1)
            act.dma_start(k_dram[:, 0:P], mid[0:H, 0, 0, 0:P]).then_inc(zeros_stored, 16)
            trig(0)
            trig(1)
            with act.Fori(2, NG) as g:
                trig(g)

            def split_high(s):
                for q in range(Q):
                    act.wait_ge(diag_ready, NB * s + CQ * (q + 1))
                    if not (isinstance(s, int) and s == 0):
                        act.wait_ge(w_used, Q * (s - 1) + q + 1)
                    cs = slice(CQ * q, CQ * (q + 1))
                    nc.scalar.copy(w_hi[:, cs, :].rearrange("p c n -> p (c n)"),
                                   w_raw[:, cs, :].rearrange("p c n -> p (c n)")).then_inc(w_hi_ready, 1)

            def gather_high(s, par):
                b = [field(act, s, f, B - 1) for f in (F_B0, F_B1)]
                if not (isinstance(s, int) and s < 2):
                    act.wait_ge(w_used, Q * (s - 1))
                for j in range(2):
                    nc.scalar.copy(z_hi[:, par, :, j * H:(j + 1) * H],
                                   z_hcb[:, :, :, bass.ds(b[j], 1)].rearrange("p c h o -> p c (h o)")
                                   ).then_inc(z_hi_ready, 1)

            def finish(s, par, t):
                act.wait_ge(w_used, Q * (s + 1))
                if not (isinstance(t, int) and t == 0):
                    act.wait_ge(stored[par], 32 * t)
                nc.scalar.copy(o_tile[:, par, 0:HALF], slot_ps[par][0][:, :]).then_inc(out_act, 1)

            def slot(s, par, t):
                gather_high(s, par)
                first = field(act, s, F_FIRST, 1)
                with act.If(first == 1):
                    split_high(s)
                with act.Else():
                    act.wait_ge(w_hi_ready, Q * s)
                    act.sem_inc(w_hi_ready, Q)
                finish(s - 1, 1 - par, t - 1 + par)

            def finish_last(m, par):
                act.wait_ge(w_used, Q * (m + 2))
                act.wait_ge(stored[par], 16 * (m + (1 - par)))
                nc.scalar.copy(o_tile[:, par, 0:HALF], slot_ps[par][0][:, :]).then_inc(out_act, 1)

            split_high(0)
            act.wait_ge(table_ready, 1)
            act.wait_ge(added, NG * NPAIR)
            gather_high(0, 0)
            slot_loop(act, slot)
            last_slot(act, finish_last)

        @block.vector
        def _(dve):
            v = nc.vector
            chain = Chain(dve, dve_step)
            link = chain.link
            steps = Chain(dve, angle_step)

            def expm1_parts(x, n):
                k, r, e = kint[:, 0:n], rest[:, 0:n], expm[:, 0:n]
                link(v.tensor_scalar(x, x, -87.0, 88.0, ALU.max, ALU.min))
                link(v.tensor_scalar(k, x, LOG2E, None, ALU.mult))
                link(v.scalar_tensor_tensor(r, k, -LN2_HI, x, ALU.mult, ALU.add))
                link(v.scalar_tensor_tensor(r, k, -LN2_LO, r, ALU.mult, ALU.add))
                link(v.tensor_scalar(e, r, 1.0 / math.factorial(7), None, ALU.mult))
                for d in range(6, 0, -1):
                    link(v.scalar_tensor_tensor(e, e, 1.0 / math.factorial(d), r, ALU.add, ALU.mult))
                link(v.tensor_scalar(scale2[:, 0:n], k, 127.0, float(1 << 23), ALU.add, ALU.mult))

            def reduce_angle(r, k, x, quarters, limits, last, link=link):
                if quarters is None:
                    link(v.tensor_scalar(k, x, INV_2PI, None, ALU.mult))
                else:
                    link(v.tensor_scalar(k, x, INV_2PI, quarters, ALU.mult, ALU.add))
                link(v.scalar_tensor_tensor(x, k, -TWO_PI_HI, x, ALU.mult, ALU.add))
                link(v.scalar_tensor_tensor(r, k, -TWO_PI_LO, x, ALU.mult, ALU.add))
                last(v.tensor_scalar(r, r, *limits, ALU.max, ALU.min))

            v.memset(mid[0:H, 0, 0, 0:P], 0.0).then_inc(zeros_ready, 1)
            dve.wait_ge(params_in, 16 * 10)
            expm1_parts(exponent, 2 * H)
            link(v.scalar_tensor_tensor(expd, expm, 1.0, scale2f, ALU.add, ALU.mult))
            v.scalar_tensor_tensor(dre, ea, -1.0, dt_, ALU.mult, ALU.mult).then_inc(dre_ready, 1)
            link(v.tensor_tensor(dim, a_im, dt_, ALU.mult))
            link(v.tensor_copy(phase_dim, dim))
            link(v.tensor_scalar(ang2[:, H:2 * H], dim, 0.5, None, ALU.mult))
            reduce_angle(rest, kint, ang2, None, (-PI_BELOW, PI_BELOW), lambda i: i.then_inc(angles2, 1))
            dve.wait_ge(consts, NCONST + 1)

            def angles(g):
                steps.turn(4 * g)
                if not (isinstance(g, int) and g == 0):
                    dve.wait_ge(sine_ready, g)
                steps.link(v.tensor_tensor(phase[:, :, :, :],
                                     phase_dim[:, bass.ds(g * GH, GH)].unsqueeze(1).unsqueeze(3).to_broadcast([P, 2, GH, S]),
                                     power.rearrange("p (e s) -> p e s", e=2).unsqueeze(2).to_broadcast([P, 2, GH, S]),
                                     ALU.mult))
                flat = [a[:, :, :, :].rearrange("p e h s -> p (e h s)") for a in (phase, turns, phase)]
                reduce_angle(*flat, quarter, (lowest, highest), lambda i: i.then_inc(angle_ready, 1), steps.link)

            def factors(g):
                dve.wait_ge(sine_ready, g + 1)
                dve.wait_ge(mag_ready, 2)
                if not (isinstance(g, int) and g == 0):
                    dve.wait_ge(k_made, g)
                v.tensor_tensor(factor[:, :, :, :], sine[:, :, :, :], mag[:, :, bass.ds(g * GH, GH), :],
                                ALU.mult).then_inc(factor_ready, 1)

            def k_rows_out(g):
                dve.wait_ge(k_made, g + 1)
                dve.wait_ge(skip_ready, g + 1)
                if not (isinstance(g, int) and g == 0):
                    dve.wait_ge(k_stored, 16 * g)
                v.tensor_tensor(k_tile[:, :, :].rearrange("a h b -> a (h b)"), k_ps[0:S, 0:GH * S],
                                k_skip[:, :, :].rearrange("a h b -> a (h b)"), ALU.add).then_inc(k_out, 1)

            def mask_pair(g, k):
                n = g * NPAIR + k
                dve.wait_ge(conv_done, n + 1)
                if not (isinstance(n, int) and n < 2):
                    dve.wait_ge(added, n - 1)
                v.tensor_tensor(mid[:, k % 2, :, :], conv_ps[k][:, :].rearrange("p (e n) -> p e n", e=2),
                                mask[:, :, :].rearrange("p c b -> p (c b)").unsqueeze(1).to_broadcast([P, 2, COL]),
                                ALU.mult).then_inc(masked, 1)

            angles(0)

            dve.wait_ge(sin2_ready, 1)
            link(v.tensor_copy(tmp_a, dre))
            expm1_parts(tmp_a, H)
            e, sc = expm[:, 0:H], scale2f[:, 0:H]
            link(v.tensor_tensor(e, e, sc, ALU.mult))
            link(v.scalar_tensor_tensor(e, sc, -1.0, e, ALU.add, ALU.add))
            half_sin, full_sin = sin2[:, H:2 * H], sin2[:, 0:H]
            link(v.scalar_tensor_tensor(tmp_a, half_sin, -2.0, half_sin, ALU.mult, ALU.mult))
            link(v.scalar_tensor_tensor(tmp_a, e, 1.0, tmp_a, ALU.add, ALU.mult))
            link(v.tensor_tensor(e_re, e, tmp_a, ALU.add))
            link(v.scalar_tensor_tensor(e_im, e, 1.0, full_sin, ALU.add, ALU.mult))

            def cross(out_, a, b, c, d, op):
                link(v.tensor_tensor(tmp_a, a, b, ALU.mult))
                link(v.tensor_tensor(tmp_b, c, d, ALU.mult))
                link(v.tensor_tensor(out_, tmp_a, tmp_b, op))

            cross(n_re, c_re, e_re, c_im, e_im, ALU.subtract)
            cross(n_im, c_re, e_im, c_im, e_re, ALU.add)
            cross(e, ea, ea, a_im, a_im, ALU.add)
            link(v.reciprocal(e, e))
            cross(alpha, n_im, a_im, n_re, ea, ALU.subtract)
            link(v.tensor_tensor(alpha, alpha, e, ALU.mult))
            link(v.tensor_scalar(alpha, alpha, sign, None, ALU.mult))
            cross(beta, n_im, ea, n_re, a_im, ALU.add)
            v.scalar_tensor_tensor(beta, beta, 2.0, e, ALU.mult, ALU.mult).then_inc(coef_ready, 1)

            dve.wait_ge(control_in, 16 * 3)
            link(v.tensor_scalar(wrap, ids_i, 0.0, float(NA), ALU.is_lt, ALU.mult))
            link(v.tensor_tensor(ids, ids_i, wrap, ALU.add))
            link(v.tensor_scalar(ids, ids, 0.0, NA - 1.0, ALU.max, ALU.min))
            link(v.tensor_scalar(same, ids[:, 0:B], own, None, ALU.is_equal))
            link(v.tensor_tensor(same, same, below, ALU.mult))
            link(v.reduce_sum(rank, same, AX))
            is_a3 = is_a.rearrange("p (a b) -> p a b", a=NA)
            link(v.tensor_tensor(is_a3, ids[:, 0:B].unsqueeze(1).to_broadcast([B, NA, B]),
                                 iota_a.unsqueeze(2).to_broadcast([B, NA, B]), ALU.is_equal))
            link(v.reduce_sum(count, is_a3, AX))
            link(v.tensor_scalar(pairs_i, count, 0.5, 0.25, ALU.mult, ALU.add))
            link(v.tensor_scalar(less, iota_a, own, None, ALU.is_lt))
            link(v.tensor_tensor(less, less, pairs_i, ALU.mult))
            link(v.reduce_sum(before, less, AX))
            link(v.scalar_tensor_tensor(pos, before, 2.0, rank, ALU.mult, ALU.add))
            link(v.tensor_scalar(match, iota_pos, pos, None, ALU.is_equal))
            v.tensor_copy(values[:, 2:3], own).then_inc(slots_placed, 1)

            factors(0)
            angles(1)
            k_rows_out(0)
            factors(1)
            link(v.tensor_copy(lens, lens_i))
            v_mask = v.tensor_tensor(mask[:, :, :], lens.unsqueeze(1).to_broadcast([P, NB, B]),
                                     t_iota.unsqueeze(2).to_broadcast([P, NB, B]), ALU.is_gt)
            link(v_mask)

            dve.wait_ge(table_rows, 1)
            link(v.tensor_copy(row[0:1, 0:3, :], table_ps[0:1, 0:3 * POS].rearrange("p (f n) -> p f n", f=3)))
            there, batch, adapter = (row[0:1, f, :].rearrange("p (s j) -> p j s", j=2) for f in range(3))
            ns = SLOTS + 1
            out_t = table[0:1, :].rearrange("p (s f) -> p f s", f=FIELDS)
            change, fill = row[0:1, 3, 0:ns], row[0:1, 4, 0:ns]
            number, odd = row[0:1, 5, 0:1], row[0:1, 6, 0:1]
            link(v.memset(table[0:1, :], 0))
            link(v.memset(change, 1.0))
            link(v.tensor_tensor(change[:, 1:ns], adapter[:, 0, 1:ns], adapter[:, 0, 0:ns - 1], ALU.not_equal))
            link(v.tensor_scalar(fill, there[:, 1, :], -1.0, 1.0, ALU.mult, ALU.add))
            link(v.tensor_tensor(fill, fill, batch[:, 0, :], ALU.mult))
            link(v.reduce_sum(number, there[:, 0, :], AX))
            link(v.tensor_copy(out_t[:, F_B0, :], batch[:, 0, :]))
            link(v.tensor_tensor(out_t[:, F_B1, :], batch[:, 1, :], fill, ALU.add))
            link(v.tensor_tensor(out_t[:, F_FIRST, :], change, there[:, 0, :], ALU.mult))
            link(v.tensor_copy(out_t[:, F_ADAPTER, :], adapter[:, 0, :]))
            link(v.tensor_copy(out_t[:, F_TWO, :], there[:, 1, :]))
            link(v.tensor_copy(out_t[:, F_ACTIVE, :], there[:, 0, :]))
            link(v.tensor_scalar(out_t[:, F_NUMBER, ns - 1:ns], number, -2.0, None, ALU.add))
            link(v.tensor_scalar(out_t[:, F_ODD, ns - 1:ns], number, 0.5, -0.25, ALU.mult, ALU.add))
            link(v.tensor_copy(odd, out_t[:, F_ODD, ns - 1:ns]))
            link(v.scalar_tensor_tensor(out_t[:, F_ODD, ns - 1:ns], odd, -2.0, number, ALU.mult, ALU.add))
            v.memset(table[0:1, 6:7], 0).then_inc(table_ready, 1)
            k_rows_out(1)
            dve.wait_ge(zeros_stored, 16)

            def turn(g):
                angles(g + 2)
                mask_pair(g, 0)
                factors(g + 2)
                mask_pair(g, 1)
                mask_pair(g, 2)
                k_rows_out(g + 2)
                mask_pair(g, 3)

            turn(0)
            with dve.Fori(1, NG - 2) as g:
                turn(g)
            for k in range(NPAIR):
                mask_pair(NG - 2, k)

            def split_low(s, q):
                dve.wait_ge(w_hi_ready, Q * s + q + 1)
                cs = slice(CQ * q, CQ * (q + 1))
                v.tensor_tensor(w_lo[:, cs, :], w_raw[:, cs, :], w_hi[:, cs, :].bitcast(f32),
                                ALU.subtract).then_inc(w_lo_ready, 1)

            for k in range(NPAIR):
                mask_pair(NG - 1, k)
                split_low(0, k)

            def gather_low(s, par):
                b = [field(dve, s, f, B - 1) for f in (F_B0, F_B1)]
                dve.wait_ge(z_hi_ready, 2 * (s + 1))
                for j in range(2):
                    v.tensor_tensor(z_lo[:, par, :, j * H:(j + 1) * H],
                                    z_hcb[:, :, :, bass.ds(b[j], 1)].rearrange("p c h o -> p c (h o)"),
                                    z_hi[:, par, :, j * H:(j + 1) * H].bitcast(f32), ALU.subtract).then_inc(z_lo_ready, 1)

            def finish(s, par, t):
                dve.wait_ge(w_used, Q * (s + 1))
                if not (isinstance(t, int) and t == 0):
                    dve.wait_ge(stored[par], 32 * t)
                v.tensor_copy(o_tile[:, par, HALF:L], slot_ps[par][1][:, :]).then_inc(out_dve, 1)

            def slot(s, par, t):
                gather_low(s, par)
                first = field(dve, s, F_FIRST, 1)
                with dve.If(first == 1):
                    for q in range(Q):
                        split_low(s, q)
                with dve.Else():
                    dve.wait_ge(w_lo_ready, Q * s)
                    dve.sem_inc(w_lo_ready, Q)
                finish(s - 1, 1 - par, t - 1 + par)

            def finish_last(m, par):
                dve.wait_ge(w_used, Q * (m + 2))
                dve.wait_ge(stored[par], 16 * (m + (1 - par)))
                v.tensor_copy(o_tile[:, par, HALF:L], slot_ps[par][1][:, :]).then_inc(out_dve, 1)

            gather_low(0, 0)
            slot_loop(dve, slot)
            last_slot(dve, finish_last)

        @block.tensor
        def _(pe):
            mm = nc.tensor.matmul

            def k_rows_made(g):
                pe.wait_ge(left_ready, g + 1)
                if not (isinstance(g, int) and g == 0):
                    pe.wait_ge(k_out, g)
                for i in range(GH):
                    last = mm(k_ps[0:S, i * S:(i + 1) * S], left[:, i, :], factor[:, 1, i, :], start=True, stop=True)
                last.then_inc(k_made, 1)

            def convolve(g, k):
                pe.wait_ge(strip_in[k], 16 * (g + 1))
                if k == 0:
                    pe.wait_ge(x_rev_in_sem, 16 * (g + 1))
                if not (isinstance(g, int) and g == 0):
                    pe.wait_ge(masked, (g - 1) * NPAIR + k + 1)
                for e in range(2):
                    for d in range(NB):
                        col = (2 * k + e) * COL
                        last = mm(conv_ps[k][:, e * COL + d * B:(e + 1) * COL],
                                  strips[:, k, e, d * P:(d + 1) * P],
                                  x_rev[:, bass.ds(g % 2, 1), col:col + (NB - d) * B].rearrange("p o n -> p (o n)"),
                                  start=(d == 0), stop=(d == NB - 1))
                last.then_inc(conv_done, 1)

            pe.wait_ge(consts, NCONST + 1)
            pe.wait_ge(slots_placed, 1)
            for f in range(3):
                last = mm(table_ps[0:1, f * POS:(f + 1) * POS], values[:, f:f + 1], match, start=True, stop=True)
            last.then_inc(table_rows, 1)
            k_rows_made(0)
            k_rows_made(1)
            def turn(g):
                for k in range(3):
                    convolve(g, k)
                k_rows_made(g + 2)
                convolve(g, 3)

            turn(0)
            with pe.Fori(1, NG - 2) as g:
                turn(g)
            for g in (NG - 2, NG - 1):
                for k in range(NPAIR):
                    convolve(g, k)

            def slot(s, par, t):
                pe.wait_ge(z_lo_ready, 2 * (s + 1))
                if not (isinstance(s, int) and s < 2):
                    pe.wait_ge(out_act, s - 1)
                    pe.wait_ge(out_dve, s - 1)
                for q in range(Q):
                    pe.wait_ge(w_lo_ready, Q * s + q + 1)
                    for c in range(CQ * q, CQ * (q + 1)):
                        for left_, right in ((z_hi, w_hi), (z_hi, w_lo), (z_lo, w_hi)):
                            for half in range(2):
                                last = mm(slot_ps[par][half][:, :], left_[:, par, c, :],
                                          right[:, c, half * HALF:(half + 1) * HALF],
                                          start=(c == 0 and left_ is z_hi and right is w_hi),
                                          stop=(c == NB - 1 and left_ is z_lo))
                    last.then_inc(w_used, 1)

            pe.wait_ge(masked, NG * NPAIR)
            slot(0, 0, 0)
            slot_loop(pe, slot)


def kernel(**inputs):
    import numpy as np
    import concourse.bacc as bacc
    from concourse import mybir as mb
    from concourse.bass_utils import run_bass_kernel_spmd

    x = np.asarray(inputs["x"])
    B, H, L = x.shape
    P, GH, Q = 128, 8, 4
    NB = L // P
    log_a = np.asarray(inputs["L0_cond_log_A_real"]).T
    w = np.asarray(inputs["L1_cond_weight"])
    NA = w.shape[0]
    arrays = {
        "x": x.reshape(B, H // GH, GH, NB, P).transpose(1, 4, 2, 3, 0).reshape(H // GH, P, GH * NB * B),
        "x_rev": x.reshape(B, H // GH, GH, NB, P)[..., ::-1].transpose(1, 4, 2, 3, 0).reshape(H // GH, P, GH * NB * B),
        "ids": np.asarray(inputs["itok_B_3_7"])[None, :],
        "lens": np.asarray(inputs["itok_B_8_3872"])[None, :],
        "log_dt": np.asarray(inputs["L0_cond_log_dt"])[None, :],
        "log_a": log_a,
        "a_imag": np.asarray(inputs["L0_cond_A_imag"]).T,
        "c": np.asarray(inputs["L0_cond_C"]).transpose(2, 1, 0),
        "d": np.asarray(inputs["L0_cond_D"])[None, :],
        "w": w.reshape(NA, L, Q, NB // Q, P).transpose(0, 2, 4, 3, 1).reshape(NA, Q, P, NB // Q * L),
    }
    arrays = {k: np.ascontiguousarray(v) for k, v in arrays.items()}
    nc = bacc.Bacc("TRN2", target_bir_lowering=False, num_devices=1)
    args = [nc.dram_tensor(f"in_{k}", v.shape, mb.dt.from_np(v.dtype), kind="ExternalInput").ap() for k, v in arrays.items()]
    out = nc.dram_tensor("out", (B, H, L), mb.dt.float32, kind="ExternalOutput").ap()
    ssm_conv_then_adapter_kernel(nc, *args, out)
    return run_bass_kernel_spmd(nc, [{f"in_{k}": v for k, v in arrays.items()}], core_ids=[0]).results[0]["out"]
```

```python
import math
from contextlib import ExitStack

import concourse.bass as bass
from concourse import mybir


class Chain:

    def __init__(self, engine, semaphore):
        self.engine, self.semaphore, self.base, self.n = engine, semaphore, 0, 0

    def turn(self, base):
        self.base, self.n = base, 0

    def mark(self, instruction):
        self.n += 1
        instruction.then_inc(self.semaphore, 1)

    def link(self, instruction):
        self.mark(instruction)
        self.engine.wait_ge(self.semaphore, self.base + self.n)


def ssm_conv_then_adapter_kernel(nc, x_in, x_rev_in, control_in, params_in, w_in, out):
    f32, f32r, i32 = mybir.dt.float32, mybir.dt.float32r, mybir.dt.int32
    ALU = mybir.AluOpType
    ACT = mybir.ActivationFunctionType
    AX = mybir.AxisListType.X

    P = 128
    B, H, L = out.shape
    N = P // 2
    NA = w_in.shape[0]
    NB = L // P
    COL = NB * B
    GH = 8
    NG = H // GH
    NPAIR = GH // 2
    S = 32
    KROW = L + P
    Q = 4
    CQ = NB // Q
    SLOTS = (B + NA) // 2
    SURE = B // 2
    POS = 2 * (SLOTS + 1)
    FIELDS = 8
    F_B0, F_B1, F_FIRST, F_ADAPTER, F_TWO, F_ACTIVE, F_NUMBER, F_ODD = range(FIELDS)
    PEEL = 4
    HALF = L // 2
    MAG_PARTS = ((0, 2 * GH), (2 * GH, H - 2 * GH))

    INV_2PI = 1.0 / (2.0 * math.pi)
    TWO_PI_HI = 6.28125
    TWO_PI_LO = 2.0 * math.pi - TWO_PI_HI
    PI_BELOW = 3.141592
    LOG2E = 1.0 / math.log(2.0)
    LN2_HI = 0.693359375
    LN2_LO = math.log(2.0) - LN2_HI

    ctx = ExitStack()
    with ctx:
        def sem(name):
            return ctx.enter_context(nc.semaphore(name))

        def tile(where, name, shape, dt=f32):
            return where.enter_context(nc.sbuf_tensor(name, shape, dt))

        z = tile(ctx, "z", [P, H, COL])
        z_group = z[:, :, :].rearrange("p (g h) n -> p g (h n)", g=NG)
        z_pair = z[:, :, :].rearrange("p (k e) n -> p k e n", e=2)
        z_hcb = z[:, :, :].rearrange("p h (c b) -> p c h b", c=NB)
        mask = tile(ctx, "mask", [P, NB, B])
        ident = tile(ctx, "ident", [P, P])
        table = tile(ctx, "table", [1, (SLOTS + 1) * FIELDS], i32)
        w_hi = tile(ctx, "w_hi", [P, NB, L], f32r)
        with ExitStack() as early:
            tile(early, "lower_quarters_of_w_lo", [P, NB // 2, L])
            x_rev = tile(early, "x_rev", [P, 2, GH * COL])
        w_lo = tile(ctx, "w_lo", [P, NB, L], f32r)

        with ExitStack() as early:
            mag = tile(early, "mag", [P, 2, H, S])
            phase = tile(early, "phase", [P, 2, GH, S])
            turns = tile(early, "turns", [P, 2, GH, S], i32)
            sine = tile(early, "sine", [P, 2, GH, S])
            factor = tile(early, "factor", [P, 2, GH, S])
            swapped = tile(early, "swapped", [P, GH, S])
            left = tile(early, "left", [P, GH, S])
            k_tile = tile(early, "k_tile", [S, GH, S])
            k_skip = tile(early, "k_skip", [S, GH, S])
            ctl = tile(early, "ctl", [P, 1024])
        w_raw = tile(ctx, "w_raw", [P, NB, L])

        with ExitStack() as early:
            strips = tile(early, "strips", [P, NPAIR, 2, L])
            mid = tile(early, "mid", [P, 2, 2, COL])
            small = tile(early, "small", [P, 38 * H])
        z_hi = tile(ctx, "z_hi", [P, 2, NB, P], f32r)
        z_lo = tile(ctx, "z_lo", [P, 2, NB, P], f32r)
        o_tile = tile(ctx, "o_tile", [P, 2, L])

        taken = [0]

        def small_tile(n, dt=f32, parts=P):
            v = small[0:parts, taken[0]:taken[0] + n]
            taken[0] += n
            assert taken[0] <= 38 * H
            return v if dt == f32 else v.bitcast(dt)

        params = small_tile(6 * H)
        exponent = params[:, 0:2 * H]
        a_im, c_ri = params[:, 2 * H:3 * H], params[:, 3 * H:5 * H]
        c_re, c_im = c_ri[:, 0:H], c_ri[:, H:2 * H]
        d_row = params[0:S, 5 * H:6 * H]
        kint = small_tile(2 * H, i32)
        rest = small_tile(2 * H)
        expm = small_tile(2 * H)
        scale2 = small_tile(2 * H, i32)
        scale2f = scale2.bitcast(f32)
        expd = small_tile(2 * H)
        dt_, ea = expd[:, 0:H], expd[:, H:2 * H]
        dre = small_tile(H)
        dre_clamped = small_tile(H)
        ang2 = small_tile(2 * H)
        dim = ang2[:, 0:H]
        phase_dim = small_tile(H)
        angle2 = small_tile(2 * H)
        sin2 = small_tile(2 * H)
        e_ri = small_tile(2 * H)
        c_over_a = ang2
        signed = c_ri
        turned = small_tile(2 * H)
        product = small_tile(2 * H)
        crossed = small_tile(2 * H)
        inverse = small_tile(H)
        alpha = small_tile(H)
        beta = small_tile(H)
        power = small_tile(2 * S)
        cols = small_tile(5)
        quarter, halfpi, sign, lowest, highest = (cols[:, i:i + 1] for i in range(5))
        corner = small_tile(S, parts=S)
        t_iota = small_tile(NB)

        at = [0]

        def ctl_tile(n, dt=f32, parts=B):
            v = ctl[0:parts, at[0]:at[0] + n]
            at[0] += n
            assert at[0] <= 1024
            return v if dt == f32 else v.bitcast(dt)

        control = ctl_tile(2 * B + 1, i32, P)
        lens_i, ids_i = control[:, 0:B], control[0:B, B:2 * B + 1]
        lens = ctl_tile(B, parts=P)
        ids = ctl_tile(B + 1)
        wrap = ctl_tile(B + 1)
        own = ids[:, B:B + 1]
        below = ctl_tile(B)
        same = ctl_tile(B)
        rank = ctl_tile(1)
        iota_a = ctl_tile(NA)
        is_a = ctl_tile(NA * B)
        count = ctl_tile(NA)
        pairs_i = ctl_tile(NA, i32)
        less = ctl_tile(NA)
        before = ctl_tile(1)
        pos = ctl_tile(1)
        iota_pos = ctl_tile(POS)
        match = ctl_tile(POS)
        values = ctl_tile(3)
        row = ctl_tile(7 * POS)[0:1, :].rearrange("p (f n) -> p f n", f=7)

        banks = [ctx.enter_context(nc.psum_tensor(f"bank{i}", [P, 512], f32)) for i in range(6)]
        conv_ps = banks[0:NPAIR]
        k_ps = banks[4]
        table_ps = banks[5]
        slot_ps = [[banks[0], banks[1]], [banks[2], banks[3]]]

        k_dram = nc.dram_tensor("k_padded", [H, KROW], f32, kind="Internal")
        k_strips = bass.AP(tensor=k_dram, offset=1, ap=[[2 * KROW, H // 2], [1, P], [KROW, 2], [1, L]])
        k_rows = k_dram[:, P:KROW].rearrange("(g h) (a b) -> g a h b", g=NG, a=S)

        params_loaded = sem("params_loaded")
        control_loaded = sem("control_loaded")
        x_in_sem, x_rev_in_sem = sem("x_loaded"), sem("x_rev_loaded")
        consts = sem("consts")
        dve_step, pool_step = sem("dve_step"), sem("pool_step")
        dre_ready = sem("dre_ready")
        e_ready = sem("e_ready")
        mag_ready = sem("mag_ready")
        angles2 = sem("angles2")
        sin2_ready = sem("sin2_ready")
        coef_ready = sem("coef_ready")
        slots_placed = sem("slots_placed")
        table_rows, table_ready = sem("table_rows"), sem("table_ready")
        angle_step = sem("angle_step")
        angle_ready, sine_ready = sem("angle_ready"), sem("sine_ready")
        factor_ready, swap_ready = sem("factor_ready"), sem("swap_ready")
        left_ready = sem("left_ready")
        skip_ready = sem("skip_ready")
        k_made, k_out = sem("k_made"), sem("k_out")
        k_stored = sem("k_stored")
        zeros_ready, zeros_stored = sem("zeros_ready"), sem("zeros_stored")
        strip_in = [sem(f"strip_in{k}") for k in range(NPAIR)]
        conv_done = sem("conv_done")
        masked = sem("masked")
        added, added_last = sem("added"), sem("added_last")
        early_hi_ready, early_lo_ready = sem("early_hi_ready"), sem("early_lo_ready")
        raw_in = [sem(f"raw_in{q}") for q in range(Q)]
        diag_ready = sem("diag_ready")
        w_hi_ready, w_lo_ready = sem("w_hi_ready"), sem("w_lo_ready")
        w_used = sem("w_used")
        z_hi_ready, z_lo_ready = sem("z_hi_ready"), sem("z_lo_ready")
        out_act, out_dve = sem("out_act"), sem("out_dve")
        stored = [sem("stored0"), sem("stored1")]
        all_stored = sem("all_stored")

        NCONST = 16

        block = ctx.enter_context(nc.Block())

        def field(engine, s, f, top):
            return engine.value_load(table[0:1, bass.ds(s * FIELDS + f, 1)], min_val=0, max_val=top)

        def slot_loop(engine, body):
            for s in range(1, PEEL):
                body(s, s % 2, s // 2)
            with engine.Fori(PEEL // 2, SURE // 2) as t:
                for par in range(2):
                    body(2 * t + par, par, t)
            with engine.Fori(SURE // 2, SLOTS // 2) as t:
                for par in range(2):
                    active = field(engine, 2 * t + par, F_ACTIVE, 1)
                    with engine.If(active == 1):
                        body(2 * t + par, par, t)

        def last_slot(engine, body):
            but_two = engine.value_load(table[0:1, SLOTS * FIELDS + F_NUMBER:SLOTS * FIELDS + F_NUMBER + 1],
                                  min_val=SURE - 2, max_val=SLOTS - 2)
            odd = field(engine, SLOTS, F_ODD, 1)
            with engine.If(odd == 1):
                body(but_two, 0)
            with engine.Else():
                body(but_two, 1)

        @block.sync
        def _(sp):
            sp.dma_start(params, params_in).then_inc(params_loaded, 16)
            sp.dma_start(control, control_in).then_inc(control_loaded, 16)

            def load_x(g):
                if not (isinstance(g, int) and g == 0):
                    sp.wait_ge(x_rev_in_sem, 16 * g)
                    sp.wait_ge(x_in_sem, 16 * g)
                if not (isinstance(g, int) and g < 2):
                    sp.wait_ge(conv_done, (g - 1) * NPAIR)
                sp.dma_start(x_rev[:, bass.ds(g % 2, 1), :].rearrange("p o n -> p (o n)"),
                             x_rev_in[bass.ds(g, 1)].rearrange("o p n -> (o p) n")).then_inc(x_rev_in_sem, 16)
                sp.dma_start(z_group[:, bass.ds(g, 1), :].rearrange("p o n -> p (o n)"),
                             x_in[bass.ds(g, 1)].rearrange("o p n -> (o p) n")).then_inc(x_in_sem, 16)

            load_x(0)
            load_x(1)

            def load_strips(g, k):
                if not (isinstance(g, int) and g == 0):
                    sp.wait_ge(conv_done, (g - 1) * NPAIR + k + 1)
                sp.dma_start(strips[:, k, :, :],
                             k_strips[bass.ds(g * NPAIR + k, 1)].rearrange("o j e m -> (o j) e m")
                             ).then_inc(strip_in[k], 16)

            def load_weights(s, adapter, q):
                if not (isinstance(s, int) and s == 0):
                    sp.wait_ge(w_lo_ready, Q * (s - 1) + q + 1)
                sp.dma_start(w_raw[:, CQ * q:CQ * (q + 1), :].rearrange("p c n -> p (c n)"),
                             w_in[bass.ds(adapter, 1), q].rearrange("o p n -> (o p) n")
                             ).then_inc(raw_in[q], 16)

            def strips_of_group(g):
                sp.wait_ge(k_stored, 16 * (g + 1))
                for k in range(NPAIR):
                    load_strips(g, k)

            sp.wait_ge(zeros_stored, 16)
            strips_of_group(0)
            with sp.Fori(1, NG - 1) as g:
                strips_of_group(g)
                load_x(g + 1)
            sp.wait_ge(k_stored, 16 * NG)
            sp.wait_ge(table_ready, 1)
            first_adapter = field(sp, 0, F_ADAPTER, NA - 1)
            for k in range(NPAIR):
                load_strips(NG - 1, k)
                load_weights(0, first_adapter, k)

            def weights_ahead(s):
                first = field(sp, s, F_FIRST, 1)
                adapter = field(sp, s, F_ADAPTER, NA - 1)
                with sp.If(first == 1):
                    for q in range(Q):
                        load_weights(s, adapter, q)
                with sp.Else():
                    for q in range(Q):
                        sp.wait_ge(raw_in[q], 16 * s)
                        sp.sem_inc(raw_in[q], 16)

            def store_slot(s, par):
                b0 = field(sp, s, F_B0, B - 1)
                b1 = field(sp, s, F_B1, B - 1)
                two = field(sp, s, F_TWO, 1)
                sp.wait_ge(out_act, s + 1)
                sp.wait_ge(out_dve, s + 1)
                sp.dma_start(out[bass.ds(b0, 1)].rearrange("o h n -> (o h) n"),
                             o_tile[0:H, par, :]).then_inc(stored[par], 16)
                sp.dma_start(out[bass.ds(b1, 1)].rearrange("o h n -> (o h) n"),
                             o_tile[H:P, par, :], cond=two == 1).then_inc(stored[par], 16)

            def slot(s, par, t):
                weights_ahead(s + 1)
                store_slot(s - 1, 1 - par)

            def finish_last(m, par):
                store_slot(m + 1, par)
                for parity, value in ((par, 16 * (m + 3 - par)), (1 - par, 16 * (m + 1 + par))):
                    sp.wait_ge(stored[parity], value)
                    sp.sem_inc(all_stored, 1)

            weights_ahead(1)
            slot_loop(sp, slot)
            last_slot(sp, finish_last)
            sp.wait_ge(all_stored, 2)

        @block.gpsimd
        def _(pool):
            chain = Chain(pool, pool_step)
            constant = Chain(pool, consts)
            constant.link(nc.gpsimd.memset(quarter[0:N, :], 0.25))
            constant.link(nc.gpsimd.memset(quarter[N:P, :], 0.0))
            constant.link(nc.gpsimd.memset(halfpi[0:N, :], math.pi / 2))
            constant.link(nc.gpsimd.memset(halfpi[N:P, :], 0.0))
            constant.link(nc.gpsimd.memset(sign[0:N, :], 2.0))
            constant.link(nc.gpsimd.memset(lowest[0:N, :], -PI_BELOW - math.pi / 2))
            constant.link(nc.gpsimd.memset(lowest[N:P, :], -PI_BELOW))
            constant.link(nc.gpsimd.memset(highest[0:N, :], PI_BELOW - math.pi / 2))
            constant.link(nc.gpsimd.memset(highest[N:P, :], PI_BELOW))
            constant.link(nc.gpsimd.memset(sign[N:P, :], -2.0))
            exact = dict(allow_small_or_imprecise_dtypes=True)
            constant.link(nc.gpsimd.iota(power[:, 0:S], [[S, S]], base=0, channel_multiplier=0, **exact))
            constant.link(nc.gpsimd.iota(power[:, S:2 * S], [[1, S]], base=0, channel_multiplier=0, **exact))
            constant.link(nc.gpsimd.iota(t_iota, [[P, NB]], base=0, channel_multiplier=1, **exact))
            constant.link(nc.gpsimd.iota(iota_a, [[1, NA]], base=0, channel_multiplier=0, **exact))
            constant.link(nc.gpsimd.iota(iota_pos, [[1, POS]], base=0, channel_multiplier=0, **exact))
            constant.link(nc.gpsimd.iota(values[:, 1:2], [[1, 1]], base=0, channel_multiplier=1, **exact))
            chain.link(nc.gpsimd.memset(corner, 1.0))
            chain.link(nc.gpsimd.affine_select(out=corner, in_=corner, compare_op=ALU.is_equal, fill=0.0,
                                               base=0, pattern=[[1, S]], channel_multiplier=S))
            chain.link(nc.gpsimd.memset(below, 1.0))
            chain.link(nc.gpsimd.affine_select(out=below, in_=below, compare_op=ALU.is_gt, fill=0.0,
                                               base=0, pattern=[[-1, B]], channel_multiplier=1))
            chain.link(nc.gpsimd.memset(ident[:, :], 1.0))
            chain.link(nc.gpsimd.affine_select(out=ident[:, :], in_=ident[:, :], compare_op=ALU.is_equal, fill=0.0,
                                               base=0, pattern=[[-1, P]], channel_multiplier=1))
            constant.link(nc.gpsimd.memset(values[:, 0:1], 1.0))
            pool.wait_ge(dre_ready, 1)
            for h, n in MAG_PARTS:
                nc.gpsimd.tensor_tensor(mag[:, :, h:h + n, :],
                                        dre[:, h:h + n].unsqueeze(1).unsqueeze(3).to_broadcast([P, 2, n, S]),
                                        power.rearrange("p (e s) -> p e s", e=2).unsqueeze(2).to_broadcast([P, 2, n, S]),
                                        ALU.mult).then_inc(e_ready, 1)
            pool.wait_ge(params_loaded, 16)
            pool.wait_ge(coef_ready, 2)

            base = chain.n
            PER = 2

            def left_factor(g):
                chain.turn(base + PER * g)
                pool.wait_ge(factor_ready, g + 1)
                if not (isinstance(g, int) and g == 0):
                    pool.wait_ge(k_made, g)
                chain.link(nc.gpsimd.tensor_tensor(left[:, :, :], factor[:, 0, :, :],
                                                   alpha[:, bass.ds(g * GH, GH)].unsqueeze(2).to_broadcast([P, GH, S]),
                                                   ALU.mult))
                pool.wait_ge(swap_ready, 2 * (g + 1))
                chain.link(nc.gpsimd.tensor_tensor(swapped[:, :, :], swapped[:, :, :],
                                                   beta[:, bass.ds(g * GH, GH)].unsqueeze(2).to_broadcast([P, GH, S]),
                                                   ALU.mult))
                nc.gpsimd.tensor_tensor(left[:, :, :], left[:, :, :], swapped[:, :, :], ALU.add).then_inc(left_ready, 1)
                if not (isinstance(g, int) and g == 0):
                    pool.wait_ge(k_out, g)
                nc.gpsimd.tensor_tensor(k_skip[:, :, :], d_row[:, bass.ds(g * GH, GH)].unsqueeze(2).to_broadcast([S, GH, S]),
                                        corner.unsqueeze(1).to_broadcast([S, GH, S]), ALU.mult).then_inc(skip_ready, 1)

            def add_masked(g, pairs=range(NPAIR)):
                pool.wait_ge(x_in_sem, 16 * (g + 1))
                for k in pairs:
                    n = g * NPAIR + k
                    pool.wait_ge(masked, n + 1)
                    nc.gpsimd.tensor_tensor(z_pair[:, bass.ds(n, 1)].rearrange("p o e n -> p (o e n)"),
                                            z_pair[:, bass.ds(n, 1)].rearrange("p o e n -> p (o e n)"),
                                            mid[:, k % 2, :, :].rearrange("p e n -> p (e n)"), ALU.add).then_inc(added, 1)

            left_factor(0)
            left_factor(1)
            with pool.Fori(0, NG - 2) as g:
                left_factor(g + 2)
                add_masked(g)
            add_masked(NG - 2)

            def add_identity(s, quarters=range(Q)):
                for q in quarters:
                    pool.wait_ge(raw_in[q], 16 * (s + 1))
                    for c in range(CQ * q, CQ * (q + 1)):
                        nc.gpsimd.tensor_tensor(w_raw[:, c, c * P:(c + 1) * P], w_raw[:, c, c * P:(c + 1) * P],
                                                ident[:, :], ALU.add).then_inc(diag_ready, 1)

            add_identity(0, [0])
            add_masked(NG - 1, [0])
            add_identity(0, [1])
            add_masked(NG - 1, [1, 2])
            add_identity(0, [2, 3])

            def slot(s):
                first = field(pool, s, F_FIRST, 1)
                with pool.If(first == 1):
                    add_identity(s)
                with pool.Else():
                    pool.wait_ge(diag_ready, NB * s)
                    pool.sem_inc(diag_ready, NB)

            pool.wait_ge(table_ready, 1)
            with pool.Fori(1, SLOTS) as s:
                slot(s)

        @block.scalar
        def _(act):
            def magnitudes(part):
                act.wait_ge(e_ready, part + 1)
                h, n = MAG_PARTS[part]
                nc.scalar.activation(mag[:, :, h:h + n, :], mag[:, :, h:h + n, :], ACT.Exp).then_inc(mag_ready, 1)

            magnitudes(0)
            act.wait_ge(angles2, 1)
            nc.scalar.activation(sin2, angle2, ACT.Sin).then_inc(sin2_ready, 1)

            def sines(g):
                act.wait_ge(angle_ready, g + 1)
                if not (isinstance(g, int) and g == 0):
                    act.wait_ge(factor_ready, g)
                nc.scalar.activation(sine[:, :, :, :].rearrange("p e h s -> p (e h s)"),
                                     phase[:, :, :, :].rearrange("p e h s -> p (e h s)"),
                                     ACT.Sin, bias=halfpi).then_inc(sine_ready, 1)

            def exchange(g):
                act.wait_ge(factor_ready, g + 1)
                if not (isinstance(g, int) and g == 0):
                    act.wait_ge(left_ready, g)
                nc.scalar.copy(swapped[0:N, :, :], factor[N:P, 0, :, :]).then_inc(swap_ready, 1)
                nc.scalar.copy(swapped[N:P, :, :], factor[0:N, 0, :, :]).then_inc(swap_ready, 1)

            def store_k(g):
                act.wait_ge(k_out, g + 1)
                act.dma_start(k_rows[g] if isinstance(g, int) else k_rows[bass.ds(g, 1)].rearrange("o a h b -> (o a) h b"),
                              k_tile[:, :, :]).then_inc(k_stored, 16)

            sines(0)
            act.wait_ge(zeros_ready, 1)
            act.dma_start(k_dram[:, 0:P], mid[0:H, 0, 0, 0:P]).then_inc(zeros_stored, 16)
            exchange(0)
            sines(1)
            store_k(0)
            exchange(1)
            magnitudes(1)
            store_k(1)
            with act.Fori(2, NG) as g:
                sines(g)
                exchange(g)
                store_k(g)

            def split_high(s, quarters=range(Q)):
                for q in quarters:
                    act.wait_ge(diag_ready, NB * s + CQ * (q + 1))
                    if not (isinstance(s, int) and s == 0):
                        act.wait_ge(w_used, Q * (s - 1) + q + 1)
                    cs = slice(CQ * q, CQ * (q + 1))
                    nc.scalar.copy(w_hi[:, cs, :].rearrange("p c n -> p (c n)"),
                                   w_raw[:, cs, :].rearrange("p c n -> p (c n)")).then_inc(w_hi_ready, 1)

            def high_parts(b, par, channels, done):
                for j in range(2):
                    nc.scalar.copy(z_hi[:, par, :, j * H + channels.start:j * H + channels.stop],
                                   z_hcb[:, :, channels, bass.ds(b[j], 1)].rearrange("p c h o -> p c (h o)")
                                   ).then_inc(done, 1)

            def gather_high(s, par):
                b = [field(act, s, f, B - 1) for f in (F_B0, F_B1)]
                if not (isinstance(s, int) and s < 2):
                    act.wait_ge(w_used, Q * (s - 1))
                high_parts(b, par, slice(0, H), z_hi_ready)

            def finish(s, par, t):
                act.wait_ge(w_used, Q * (s + 1))
                if not (isinstance(t, int) and t == 0):
                    act.wait_ge(stored[par], 32 * t)
                nc.scalar.copy(o_tile[:, par, 0:HALF], slot_ps[par][0][:, :]).then_inc(out_act, 1)

            def slot(s, par, t):
                gather_high(s, par)
                first = field(act, s, F_FIRST, 1)
                with act.If(first == 1):
                    split_high(s)
                with act.Else():
                    act.wait_ge(w_hi_ready, Q * s)
                    act.sem_inc(w_hi_ready, Q)
                finish(s - 1, 1 - par, t - 1 + par)

            def finish_last(m, par):
                act.wait_ge(w_used, Q * (m + 2))
                act.wait_ge(stored[par], 16 * (m + (1 - par)))
                nc.scalar.copy(o_tile[:, par, 0:HALF], slot_ps[par][0][:, :]).then_inc(out_act, 1)

            split_high(0, [0])
            act.wait_ge(table_ready, 1)
            first_slot = [field(act, 0, f, B - 1) for f in (F_B0, F_B1)]
            act.wait_ge(added, (NG - 1) * NPAIR)
            act.wait_ge(conv_done, (NG - 1) * NPAIR + 2)
            high_parts(first_slot, 0, slice(0, H - GH), early_hi_ready)
            split_high(0, [1])
            act.wait_ge(added, NG * NPAIR - 1)
            act.wait_ge(added_last, 1)
            high_parts(first_slot, 0, slice(H - GH, H), z_hi_ready)
            split_high(0, [2, 3])
            slot_loop(act, slot)
            last_slot(act, finish_last)

        @block.vector
        def _(dve):
            v = nc.vector
            chain = Chain(dve, dve_step)
            link = chain.link
            steps = Chain(dve, angle_step)

            def expm1_parts(x, n):
                k, r, e = kint[:, 0:n], rest[:, 0:n], expm[:, 0:n]
                link(v.tensor_scalar(x, x, -87.0, 88.0, ALU.max, ALU.min))
                link(v.tensor_scalar(k, x, LOG2E, None, ALU.mult))
                link(v.scalar_tensor_tensor(r, k, -LN2_HI, x, ALU.mult, ALU.add))
                link(v.scalar_tensor_tensor(r, k, -LN2_LO, r, ALU.mult, ALU.add))
                link(v.tensor_scalar(e, r, 1.0 / math.factorial(7), None, ALU.mult))
                for d in range(6, 0, -1):
                    link(v.scalar_tensor_tensor(e, e, 1.0 / math.factorial(d), r, ALU.add, ALU.mult))
                link(v.tensor_scalar(scale2[:, 0:n], k, 127.0, float(1 << 23), ALU.add, ALU.mult))

            def reduce_angle(r, k, x, quarters, limits, last, link=link):
                if quarters is None:
                    link(v.tensor_scalar(k, x, INV_2PI, None, ALU.mult))
                else:
                    link(v.tensor_scalar(k, x, INV_2PI, quarters, ALU.mult, ALU.add))
                link(v.scalar_tensor_tensor(x, k, -TWO_PI_HI, x, ALU.mult, ALU.add))
                link(v.scalar_tensor_tensor(r, k, -TWO_PI_LO, x, ALU.mult, ALU.add))
                last(v.tensor_scalar(r, r, *limits, ALU.max, ALU.min))

            v.memset(mid[0:H, 0, 0, 0:P], 0.0).then_inc(zeros_ready, 1)
            dve.wait_ge(params_loaded, 16)
            expm1_parts(exponent, 2 * H)
            link(v.scalar_tensor_tensor(expd, expm, 1.0, scale2f, ALU.add, ALU.mult))
            v.scalar_tensor_tensor(dre, ea, -1.0, dt_, ALU.mult, ALU.mult).then_inc(dre_ready, 1)
            link(v.tensor_tensor(dim, a_im, dt_, ALU.mult))
            chain.mark(v.tensor_copy(phase_dim, dim))
            link(v.tensor_scalar(ang2[:, H:2 * H], dim, 0.5, None, ALU.mult))
            reduce_angle(angle2, kint, ang2, None, (-PI_BELOW, PI_BELOW), lambda i: i.then_inc(angles2, 1))
            dve.wait_ge(consts, NCONST + 1)

            def angles(g):
                steps.turn(4 * g)
                if not (isinstance(g, int) and g == 0):
                    dve.wait_ge(sine_ready, g)
                steps.link(v.tensor_tensor(phase[:, :, :, :],
                                     phase_dim[:, bass.ds(g * GH, GH)].unsqueeze(1).unsqueeze(3).to_broadcast([P, 2, GH, S]),
                                     power.rearrange("p (e s) -> p e s", e=2).unsqueeze(2).to_broadcast([P, 2, GH, S]),
                                     ALU.mult))
                flat = [a[:, :, :, :].rearrange("p e h s -> p (e h s)") for a in (phase, turns, phase)]
                reduce_angle(*flat, quarter, (lowest, highest), lambda i: i.then_inc(angle_ready, 1), steps.link)

            def factors(g):
                dve.wait_ge(sine_ready, g + 1)
                dve.wait_ge(mag_ready, 1 if isinstance(g, int) and g < 2 else 2)
                if not (isinstance(g, int) and g == 0):
                    dve.wait_ge(k_made, g)
                v.tensor_tensor(factor[:, :, :, :], sine[:, :, :, :], mag[:, :, bass.ds(g * GH, GH), :],
                                ALU.mult).then_inc(factor_ready, 1)

            def k_rows_out(g):
                dve.wait_ge(k_made, g + 1)
                dve.wait_ge(skip_ready, g + 1)
                if not (isinstance(g, int) and g == 0):
                    dve.wait_ge(k_stored, 16 * g)
                v.tensor_tensor(k_tile[:, :, :].rearrange("a h b -> a (h b)"), k_ps[0:S, 0:GH * S],
                                k_skip[:, :, :].rearrange("a h b -> a (h b)"), ALU.add).then_inc(k_out, 1)

            def mask_pair(g, k):
                n = g * NPAIR + k
                dve.wait_ge(conv_done, n + 1)
                if not (isinstance(n, int) and n < 2):
                    dve.wait_ge(added, n - 1)
                v.tensor_tensor(mid[:, k % 2, :, :], conv_ps[k][:, :].rearrange("p (e n) -> p e n", e=2),
                                mask[:, :, :].rearrange("p c b -> p (c b)").unsqueeze(1).to_broadcast([P, 2, COL]),
                                ALU.mult).then_inc(masked, 1)

            angles(0)

            def halves(t):
                return t.rearrange("p (e h) -> p e h", e=2)

            def both(t):
                return t.unsqueeze(1).to_broadcast([P, 2, H])

            c_ri2, product2, crossed2 = (halves(t) for t in (c_ri, product, crossed))
            chain.mark(v.tensor_scalar(dre_clamped, dre, 1.0, None, ALU.mult))
            chain.mark(v.tensor_tensor(product[:, 0:H], ea, ea, ALU.mult))
            link(v.tensor_tensor(product[:, H:2 * H], a_im, a_im, ALU.mult))
            link(v.tensor_tensor(inverse, product[:, 0:H], product[:, H:2 * H], ALU.add))
            link(v.reciprocal(inverse, inverse))
            chain.mark(v.tensor_tensor(product2, c_ri2, both(ea), ALU.mult))
            link(v.tensor_tensor(crossed2, c_ri2, both(a_im), ALU.mult))
            chain.mark(v.tensor_tensor(c_over_a[:, 0:H], crossed[:, H:2 * H], product[:, 0:H], ALU.subtract))
            link(v.scalar_tensor_tensor(c_over_a[:, H:2 * H], crossed[:, 0:H], -1.0, product[:, H:2 * H],
                                        ALU.mult, ALU.subtract))
            link(v.tensor_tensor(halves(c_over_a), halves(c_over_a), both(inverse), ALU.mult))
            chain.mark(v.tensor_scalar(signed, c_over_a, sign, None, ALU.mult))
            chain.mark(v.tensor_scalar(turned[:, 0:H], c_over_a[:, H:2 * H], -2.0, None, ALU.mult))
            chain.mark(v.tensor_scalar(turned[:, H:2 * H], c_over_a[:, 0:H], -2.0, None, ALU.mult))

            expm1_parts(dre_clamped, H)
            e, sc = expm[:, 0:H], scale2f[:, 0:H]
            link(v.tensor_tensor(e, e, sc, ALU.mult))
            link(v.scalar_tensor_tensor(e, sc, -1.0, e, ALU.add, ALU.add))
            dve.wait_ge(sin2_ready, 1)
            half_sin, full_sin = sin2[:, H:2 * H], sin2[:, 0:H]
            chain.mark(v.scalar_tensor_tensor(e_ri[:, H:2 * H], e, 1.0, full_sin, ALU.add, ALU.mult))
            link(v.scalar_tensor_tensor(product[:, 0:H], half_sin, -2.0, half_sin, ALU.mult, ALU.mult))
            link(v.scalar_tensor_tensor(product[:, 0:H], e, 1.0, product[:, 0:H], ALU.add, ALU.mult))
            link(v.tensor_tensor(e_ri[:, 0:H], e, product[:, 0:H], ALU.add))
            chain.mark(v.tensor_tensor(product, e_ri, signed, ALU.mult))
            link(v.tensor_tensor(crossed, e_ri, turned, ALU.mult))
            v.tensor_tensor(alpha, product[:, 0:H], product[:, H:2 * H], ALU.subtract).then_inc(coef_ready, 1)
            v.tensor_tensor(beta, crossed[:, 0:H], crossed[:, H:2 * H], ALU.add).then_inc(coef_ready, 1)
            factors(0)
            angles(1)
            k_rows_out(0)
            factors(1)


            dve.wait_ge(control_loaded, 16)
            link(v.tensor_scalar(wrap, ids_i, 0.0, float(NA), ALU.is_lt, ALU.mult))
            link(v.tensor_tensor(ids, ids_i, wrap, ALU.add))
            link(v.tensor_scalar(ids, ids, 0.0, NA - 1.0, ALU.max, ALU.min))
            link(v.tensor_scalar(same, ids[:, 0:B], own, None, ALU.is_equal))
            link(v.tensor_tensor(same, same, below, ALU.mult))
            link(v.reduce_sum(rank, same, AX))
            is_a3 = is_a.rearrange("p (a b) -> p a b", a=NA)
            link(v.tensor_tensor(is_a3, ids[:, 0:B].unsqueeze(1).to_broadcast([B, NA, B]),
                                 iota_a.unsqueeze(2).to_broadcast([B, NA, B]), ALU.is_equal))
            link(v.reduce_sum(count, is_a3, AX))
            link(v.tensor_scalar(pairs_i, count, 0.5, 0.25, ALU.mult, ALU.add))
            link(v.tensor_scalar(less, iota_a, own, None, ALU.is_lt))
            link(v.tensor_tensor(less, less, pairs_i, ALU.mult))
            link(v.reduce_sum(before, less, AX))
            link(v.scalar_tensor_tensor(pos, before, 2.0, rank, ALU.mult, ALU.add))
            link(v.tensor_scalar(match, iota_pos, pos, None, ALU.is_equal))
            v.tensor_copy(values[:, 2:3], own).then_inc(slots_placed, 1)

            k_rows_out(1)
            link(v.tensor_copy(lens, lens_i))
            v_mask = v.tensor_tensor(mask[:, :, :], lens.unsqueeze(1).to_broadcast([P, NB, B]),
                                     t_iota.unsqueeze(2).to_broadcast([P, NB, B]), ALU.is_gt)
            link(v_mask)

            dve.wait_ge(table_rows, 1)
            link(v.tensor_copy(row[0:1, 0:3, :], table_ps[0:1, 0:3 * POS].rearrange("p (f n) -> p f n", f=3)))
            there, batch, adapter = (row[0:1, f, :].rearrange("p (s j) -> p j s", j=2) for f in range(3))
            ns = SLOTS + 1
            out_t = table[0:1, :].rearrange("p (s f) -> p f s", f=FIELDS)
            change, fill = row[0:1, 3, 0:ns], row[0:1, 4, 0:ns]
            number, odd = row[0:1, 5, 0:1], row[0:1, 6, 0:1]
            link(v.memset(table[0:1, :], 0))
            link(v.memset(change, 1.0))
            link(v.tensor_tensor(change[:, 1:ns], adapter[:, 0, 1:ns], adapter[:, 0, 0:ns - 1], ALU.not_equal))
            link(v.tensor_scalar(fill, there[:, 1, :], -1.0, 1.0, ALU.mult, ALU.add))
            link(v.tensor_tensor(fill, fill, batch[:, 0, :], ALU.mult))
            link(v.reduce_sum(number, there[:, 0, :], AX))
            link(v.tensor_copy(out_t[:, F_B0, :], batch[:, 0, :]))
            link(v.tensor_tensor(out_t[:, F_B1, :], batch[:, 1, :], fill, ALU.add))
            link(v.tensor_tensor(out_t[:, F_FIRST, :], change, there[:, 0, :], ALU.mult))
            link(v.tensor_copy(out_t[:, F_ADAPTER, :], adapter[:, 0, :]))
            link(v.tensor_copy(out_t[:, F_TWO, :], there[:, 1, :]))
            link(v.tensor_copy(out_t[:, F_ACTIVE, :], there[:, 0, :]))
            link(v.tensor_scalar(out_t[:, F_NUMBER, ns - 1:ns], number, -2.0, None, ALU.add))
            link(v.tensor_scalar(out_t[:, F_ODD, ns - 1:ns], number, 0.5, -0.25, ALU.mult, ALU.add))
            link(v.tensor_copy(odd, out_t[:, F_ODD, ns - 1:ns]))
            link(v.scalar_tensor_tensor(out_t[:, F_ODD, ns - 1:ns], odd, -2.0, number, ALU.mult, ALU.add))
            v.memset(table[0:1, 6:7], 0).then_inc(table_ready, 1)
            dve.wait_ge(zeros_stored, 16)

            def turn(g):
                angles(g + 2)
                mask_pair(g, 0)
                factors(g + 2)
                mask_pair(g, 1)
                mask_pair(g, 2)
                k_rows_out(g + 2)
                mask_pair(g, 3)

            turn(0)
            with dve.Fori(1, NG - 2) as g:
                turn(g)
            for k in range(NPAIR):
                mask_pair(NG - 2, k)

            def split_low(s, q):
                dve.wait_ge(w_hi_ready, Q * s + q + 1)
                cs = slice(CQ * q, CQ * (q + 1))
                v.tensor_tensor(w_lo[:, cs, :], w_raw[:, cs, :], w_hi[:, cs, :].bitcast(f32),
                                ALU.subtract).then_inc(w_lo_ready, 1)

            def low_parts(b, par, channels, done):
                for j in range(2):
                    v.tensor_tensor(z_lo[:, par, :, j * H + channels.start:j * H + channels.stop],
                                    z_hcb[:, :, channels, bass.ds(b[j], 1)].rearrange("p c h o -> p c (h o)"),
                                    z_hi[:, par, :, j * H + channels.start:j * H + channels.stop].bitcast(f32),
                                    ALU.subtract).then_inc(done, 1)

            def gather_low(s, par):
                b = [field(dve, s, f, B - 1) for f in (F_B0, F_B1)]
                dve.wait_ge(z_hi_ready, 2 * (s + 1))
                low_parts(b, par, slice(0, H), z_lo_ready)

            def finish(s, par, t):
                dve.wait_ge(w_used, Q * (s + 1))
                if not (isinstance(t, int) and t == 0):
                    dve.wait_ge(stored[par], 32 * t)
                v.tensor_copy(o_tile[:, par, HALF:L], slot_ps[par][1][:, :]).then_inc(out_dve, 1)

            def slot(s, par, t):
                gather_low(s, par)
                first = field(dve, s, F_FIRST, 1)
                with dve.If(first == 1):
                    for q in range(Q):
                        split_low(s, q)
                with dve.Else():
                    dve.wait_ge(w_lo_ready, Q * s)
                    dve.sem_inc(w_lo_ready, Q)
                finish(s - 1, 1 - par, t - 1 + par)

            def finish_last(m, par):
                dve.wait_ge(w_used, Q * (m + 2))
                dve.wait_ge(stored[par], 16 * (m + (1 - par)))
                v.tensor_copy(o_tile[:, par, HALF:L], slot_ps[par][1][:, :]).then_inc(out_dve, 1)

            mask_pair(NG - 1, 0)
            split_low(0, 0)
            mask_pair(NG - 1, 1)
            first_slot = [field(dve, 0, f, B - 1) for f in (F_B0, F_B1)]
            dve.wait_ge(early_hi_ready, 2)
            low_parts(first_slot, 0, slice(0, H - GH), early_lo_ready)
            mask_pair(NG - 1, 2)
            mask_pair(NG - 1, NPAIR - 1)
            dve.wait_ge(masked, NG * NPAIR)
            dve.wait_ge(x_in_sem, 16 * NG)
            last_pair = z_pair[:, H // 2 - 1, :, :].rearrange("p e n -> p (e n)")
            v.tensor_tensor(last_pair, last_pair, mid[:, (NPAIR - 1) % 2, :, :].rearrange("p e n -> p (e n)"),
                            ALU.add).then_inc(added_last, 1)
            dve.wait_ge(z_hi_ready, 2)
            low_parts(first_slot, 0, slice(H - GH, H), z_lo_ready)
            for q in range(1, Q):
                split_low(0, q)
            slot_loop(dve, slot)
            last_slot(dve, finish_last)

        @block.tensor
        def _(pe):
            mm = nc.tensor.matmul

            def k_rows_made(g):
                pe.wait_ge(left_ready, g + 1)
                if not (isinstance(g, int) and g == 0):
                    pe.wait_ge(k_out, g)
                for i in range(GH):
                    last = mm(k_ps[0:S, i * S:(i + 1) * S], left[:, i, :], factor[:, 1, i, :], start=True, stop=True)
                last.then_inc(k_made, 1)

            def convolve(g, k):
                pe.wait_ge(strip_in[k], 16 * (g + 1))
                if k == 0:
                    pe.wait_ge(x_rev_in_sem, 16 * (g + 1))
                if not (isinstance(g, int) and g == 0):
                    pe.wait_ge(masked, (g - 1) * NPAIR + k + 1)
                for e in range(2):
                    for d in range(NB):
                        col = (2 * k + e) * COL
                        last = mm(conv_ps[k][:, e * COL + d * B:(e + 1) * COL],
                                  strips[:, k, e, d * P:(d + 1) * P],
                                  x_rev[:, bass.ds(g % 2, 1), col:col + (NB - d) * B].rearrange("p o n -> p (o n)"),
                                  start=(d == 0), stop=(d == NB - 1))
                last.then_inc(conv_done, 1)

            k_rows_made(0)
            k_rows_made(1)
            pe.wait_ge(consts, NCONST + 1)
            pe.wait_ge(slots_placed, 1)
            for f in range(3):
                last = mm(table_ps[0:1, f * POS:(f + 1) * POS], values[:, f:f + 1], match, start=True, stop=True)
            last.then_inc(table_rows, 1)

            def turn(g):
                for k in range(3):
                    convolve(g, k)
                k_rows_made(g + 2)
                convolve(g, 3)

            turn(0)
            with pe.Fori(1, NG - 2) as g:
                turn(g)
            for g in (NG - 2, NG - 1):
                for k in range(NPAIR):
                    convolve(g, k)

            def slot(s, par, t):
                pe.wait_ge(z_lo_ready, 2 * (s + 1))
                if not (isinstance(s, int) and s < 2):
                    pe.wait_ge(out_act, s - 1)
                    pe.wait_ge(out_dve, s - 1)
                for q in range(Q):
                    pe.wait_ge(w_lo_ready, Q * s + q + 1)
                    for c in range(CQ * q, CQ * (q + 1)):
                        for left_, right in ((z_hi, w_hi), (z_hi, w_lo), (z_lo, w_hi)):
                            for half in range(2):
                                last = mm(slot_ps[par][half][:, :], left_[:, par, c, :],
                                          right[:, c, half * HALF:(half + 1) * HALF],
                                          start=(c == 0 and left_ is z_hi and right is w_hi),
                                          stop=(c == NB - 1 and left_ is z_lo))
                    last.then_inc(w_used, 1)

            pe.wait_ge(masked, NG * NPAIR)
            pe.wait_ge(early_lo_ready, 2)
            slot(0, 0, 0)
            slot_loop(pe, slot)


def kernel(**inputs):
    import numpy as np
    import concourse.bacc as bacc
    from concourse import mybir as mb
    from concourse.bass_utils import run_bass_kernel_spmd

    x = np.asarray(inputs["x"])
    B, H, L = x.shape
    P, GH, Q = 128, 8, 4
    NB = L // P
    ids, lens = np.asarray(inputs["itok_B_3_7"]), np.asarray(inputs["itok_B_8_3872"])
    log_dt, log_a, a_imag, c, d = (np.asarray(inputs["L0_cond_" + name])
                                   for name in ("log_dt", "log_A_real", "A_imag", "C", "D"))
    w = np.asarray(inputs["L1_cond_weight"])
    NA = w.shape[0]
    arrays = {
        "x": x.reshape(B, H // GH, GH, NB, P).transpose(1, 4, 2, 3, 0).reshape(H // GH, P, GH * NB * B),
        "x_rev": x.reshape(B, H // GH, GH, NB, P)[..., ::-1].transpose(1, 4, 2, 3, 0).reshape(H // GH, P, GH * NB * B),
        "control": np.concatenate([np.tile(lens, (P, 1)), np.tile(ids, (P, 1)), np.tile(ids, P // B)[:, None]], 1),
        "params": np.concatenate([np.tile(log_dt, (P, 1)), *(np.tile(m.T, (2, 1)) for m in (log_a, a_imag, c[..., 0], c[..., 1])),
                                  np.tile(d, (P, 1))], 1),
        "w": w.reshape(NA, L, Q, NB // Q, P).transpose(0, 2, 4, 3, 1).reshape(NA, Q, P, NB // Q * L),
    }
    arrays = {k: np.ascontiguousarray(v) for k, v in arrays.items()}
    nc = bacc.Bacc("TRN2", target_bir_lowering=False, num_devices=1)
    args = [nc.dram_tensor(f"in_{k}", v.shape, mb.dt.from_np(v.dtype), kind="ExternalInput").ap() for k, v in arrays.items()]
    out = nc.dram_tensor("out", (B, H, L), mb.dt.float32, kind="ExternalOutput").ap()
    ssm_conv_then_adapter_kernel(nc, *args, out)
    return run_bass_kernel_spmd(nc, [{f"in_{k}": v for k, v in arrays.items()}], core_ids=[0]).results[0]["out"]
```

```python
import math
from contextlib import ExitStack

import concourse.bass as bass
from concourse import mybir


class Chain:

    def __init__(self, engine, semaphore):
        self.engine, self.semaphore, self.base, self.n = engine, semaphore, 0, 0

    def turn(self, base):
        self.base, self.n = base, 0

    def mark(self, instruction):
        self.n += 1
        instruction.then_inc(self.semaphore, 1)

    def link(self, instruction):
        self.mark(instruction)
        self.engine.wait_ge(self.semaphore, self.base + self.n)


def ssm_conv_then_adapter_kernel(nc, x_in, control_in, params_in, w_in, out):
    f32, f32r, f16, i32 = mybir.dt.float32, mybir.dt.float32r, mybir.dt.float16, mybir.dt.int32
    ALU = mybir.AluOpType
    ACT = mybir.ActivationFunctionType
    AX = mybir.AxisListType.X

    P = 128
    B, H, L = out.shape
    N = P // 2
    NA = w_in.shape[0]
    NB = L // P
    COL = NB * B
    GH = 8
    NG = H // GH
    NPAIR = GH // 2
    S = 32
    KROW = L + P
    COPIES = 4
    RUN = P // COPIES
    Q = 4
    CQ = NB // Q
    SLOTS = (B + NA) // 2
    SURE = B // 2
    POS = 2 * (SLOTS + 1)
    FIELDS = 8
    F_B0, F_B1, F_FIRST, F_ADAPTER, F_TWO, F_ACTIVE, F_NUMBER, F_ODD = range(FIELDS)
    EARLY_QUARTERS = (2, 5)
    PEEL = 4
    HALF = L // 2
    MAG_PARTS = ((0, 2 * GH), (2 * GH, H - 2 * GH))

    INV_2PI = 1.0 / (2.0 * math.pi)
    TWO_PI_HI = 6.28125
    TWO_PI_LO = 2.0 * math.pi - TWO_PI_HI
    PI_BELOW = 3.141592
    LOG2E = 1.0 / math.log(2.0)
    LN2_HI = 0.693359375
    LN2_LO = math.log(2.0) - LN2_HI

    ctx = ExitStack()
    with ctx:
        def sem(name):
            return ctx.enter_context(nc.semaphore(name))

        def tile(where, name, shape, dt=f32):
            return where.enter_context(nc.sbuf_tensor(name, shape, dt))

        z = tile(ctx, "z", [P, H, COL])
        z_group = z[:, :, :].rearrange("p (g h) n -> p g (h n)", g=NG)
        z_pair = z[:, :, :].rearrange("p (k e) n -> p k e n", e=2)
        z_hcb = z[:, :, :].rearrange("p h (c b) -> p c h b", c=NB)
        mask = tile(ctx, "mask", [P, NB, B])
        ident = tile(ctx, "ident", [P, P])
        table = tile(ctx, "table", [1, (SLOTS + 1) * FIELDS], i32)
        with ExitStack() as early:
            tile(early, "lower_quarters_of_w_hi", [P, NB // 2, L])
            w_raw_early = tile(early, "w_raw_early", [P, NB // 2, L])
        w_hi = tile(ctx, "w_hi", [P, NB, L], f32r)
        with ExitStack() as early:
            skip_row = tile(early, "skip_row", [P, GH, S])
            k_scaled = tile(early, "k_scaled", [S, GH, S])
            ones = tile(early, "ones", [P, P])
            scratch = tile(early, "scratch", [P, 10 * H])
            magnitude = tile(early, "magnitude", [P, NPAIR, 2 * COL])
            tile(early, "rest_of_lower_quarters_of_w_lo", [P, NB // 2 * L - 2 * GH * S - P - 10 * H - NPAIR * 2 * COL])
            x16 = tile(early, "x16", [P, 2, 2, GH * COL], f16)
        w_lo = tile(ctx, "w_lo", [P, NB, L], f32r)

        with ExitStack() as early:
            mag = tile(early, "mag", [P, 2, H, S])
            phase = tile(early, "phase", [P, 2, GH, S])
            turns = tile(early, "turns", [P, 2, GH, S], i32)
            sine = tile(early, "sine", [P, 2, GH, S])
            factor = tile(early, "factor", [P, 2, GH, S])
            swapped = tile(early, "swapped", [P, GH, S])
            left = tile(early, "left", [P, GH, S])
            k_tile = tile(early, "k_tile", [S, GH, S, 2], f16)
            ctl = tile(early, "ctl", [P, 1024])
        w_raw = tile(ctx, "w_raw", [P, NB, L])

        def raw(s, q):
            if isinstance(s, int) and s == 0 and q < 2:
                return w_raw_early[:, CQ * (1 - q):CQ * (2 - q), :]
            return w_raw[:, CQ * q:CQ * (q + 1), :]

        with ExitStack() as early:
            strips = tile(early, "strips", [P, NPAIR, 2, L])
            mid = tile(early, "mid", [P, 2, 2, COL])
            small = tile(early, "small", [P, 38 * H])
        strips16 = strips[:, :, :, :].bitcast(f16).rearrange("p k e (d m two) -> p k e two d m", two=2, d=NB)
        z_hi = tile(ctx, "z_hi", [P, 2, NB, P], f32r)
        z_lo = tile(ctx, "z_lo", [P, 2, NB, P], f32r)
        o_tile = tile(ctx, "o_tile", [P, 2, L])

        taken = [0]

        def small_tile(n, dt=f32, parts=P):
            v = small[0:parts, taken[0]:taken[0] + n]
            taken[0] += n
            assert taken[0] <= 38 * H
            return v if dt == f32 else v.bitcast(dt)

        params = small_tile(6 * H)
        exponent = params[:, 0:2 * H]
        a_im, c_ri = params[:, 2 * H:3 * H], params[:, 3 * H:5 * H]
        c_re, c_im = c_ri[:, 0:H], c_ri[:, H:2 * H]
        d_row = params[:, 5 * H:6 * H]
        kint, scale2 = (scratch[:, 2 * i * H:2 * (i + 1) * H].bitcast(i32) for i in (0, 1))
        rest, expm, expd = (scratch[:, 2 * i * H:2 * (i + 1) * H] for i in (2, 3, 4))
        scale2f = scale2.bitcast(f32)
        dt_, ea = expd[:, 0:H], expd[:, H:2 * H]
        dre = small_tile(H)
        dre_clamped = small_tile(H)
        ang2 = small_tile(2 * H)
        dim = ang2[:, 0:H]
        phase_dim = small_tile(H)
        angle2 = small_tile(2 * H)
        sin2 = small_tile(2 * H)
        e_ri = small_tile(2 * H)
        c_over_a = ang2
        signed = c_ri
        turned = small_tile(2 * H)
        product = small_tile(2 * H)
        crossed = small_tile(2 * H)
        inverse = small_tile(H)
        alpha_beta = small_tile(2 * H)
        alpha, beta = alpha_beta[:, 0:H], alpha_beta[:, H:2 * H]
        k_scale_i, k_inverse_i = small_tile(H, i32), small_tile(H, i32)
        k_scale, k_inverse = k_scale_i.bitcast(f32), k_inverse_i.bitcast(f32)
        x_scale_i, x_inverse_i = small_tile(NG, i32), small_tile(NG, i32)
        x_scale, x_inverse = x_scale_i.bitcast(f32), x_inverse_i.bitcast(f32)
        xk_inverse = small_tile(H)
        x_exponent = small_tile(2, i32)
        x_sums = small_tile(NPAIR)
        x_bound = small_tile(1)
        power = small_tile(2 * S)
        cols = small_tile(5)
        quarter, halfpi, sign, lowest, highest = (cols[:, i:i + 1] for i in range(5))
        corner = small_tile(S)
        t_iota = small_tile(NB)
        least_adapter = small_tile(1, i32, 1)

        at = [0]

        def ctl_tile(n, dt=f32, parts=B):
            v = ctl[0:parts, at[0]:at[0] + n]
            at[0] += n
            assert at[0] <= 1024
            return v if dt == f32 else v.bitcast(dt)

        control = ctl_tile(2 * B + 1, i32, P)
        lens_i, ids_i = control[:, 0:B], control[0:B, B:2 * B + 1]
        lens = ctl_tile(B, parts=P)
        ids = ctl_tile(B + 1)
        wrap = ctl_tile(B + 1)
        own = ids[:, B:B + 1]
        below = ctl_tile(B)
        same = ctl_tile(B)
        rank = ctl_tile(1)
        iota_a = ctl_tile(NA)
        is_a = ctl_tile(NA * B)
        count = ctl_tile(NA)
        pairs_i = ctl_tile(NA, i32)
        less = ctl_tile(NA)
        before = ctl_tile(1)
        pos = ctl_tile(1)
        iota_pos = ctl_tile(POS)
        match = ctl_tile(POS)
        values = ctl_tile(3)
        row = ctl_tile(7 * POS)[0:1, :].rearrange("p (f n) -> p f n", f=7)

        banks = [ctx.enter_context(nc.psum_tensor(f"bank{i}", [P, 512], f32)) for i in range(8)]
        conv_ps = banks[0:NPAIR]
        k_ps = banks[4]
        table_ps = banks[5]
        k_bound_ps, x_bound_ps = banks[6][:, 0:H], banks[7][:, 0:NPAIR]
        slot_ps = [[banks[0], banks[1]], [banks[2], banks[3]]]

        k_dram = nc.dram_tensor("k_padded", [H, COPIES, KROW], f32, kind="Internal")
        k_rows = k_dram[:, :, P:KROW].rearrange("(g h) q (a b) -> g q a h b", g=NG, a=S)

        def strip_source(h):
            return bass.AP(tensor=k_dram, offset=h * COPIES * KROW + P, ap=[[KROW - RUN, COPIES], [-1, RUN], [1, L]])

        params_loaded = sem("params_loaded")
        control_loaded = sem("control_loaded")
        x_arrived = [sem("x_arrived0"), sem("x_arrived1")]
        x_loaded = sem("x_loaded")
        consts = sem("consts")
        dve_step, pool_step = sem("dve_step"), sem("pool_step")
        dre_ready = sem("dre_ready")
        e_ready = sem("e_ready")
        mag_ready = sem("mag_ready")
        angles2 = sem("angles2")
        sin2_ready = sem("sin2_ready")
        coef_ready = sem("coef_ready")
        least_ready, slots_placed = sem("least_ready"), sem("slots_placed")
        table_rows, table_ready = sem("table_rows"), sem("table_ready")
        angle_step = sem("angle_step")
        angle_ready, sine_ready = sem("angle_ready"), sem("sine_ready")
        factor_ready, swap_ready = sem("factor_ready"), sem("swap_ready")
        left_ready = sem("left_ready")
        skip_ready = sem("skip_ready")
        bound_ready, k_bound_summed = sem("bound_ready"), sem("k_bound_summed")
        x_sums_ready, x_bound_summed = sem("x_sums_ready"), sem("x_bound_summed")
        scale_step = sem("scale_step")
        x_scale_ready, x_hi_ready, x_lo_ready = sem("x_scale_ready"), sem("x_hi_ready"), sem("x_lo_ready")
        k_made, k_scaled_ready = sem("k_made"), sem("k_scaled_ready")
        k_hi_ready, k_out = sem("k_hi_ready"), sem("k_out")
        k_stored = sem("k_stored")
        zeros_ready, zeros_stored = sem("zeros_ready"), sem("zeros_stored")
        strip_in = [[sem(f"strip_in{k}_{e}") for e in range(2)] for k in range(NPAIR)]
        conv_done = sem("conv_done")
        masked = sem("masked")
        added, added_last = sem("added"), sem("added_last")
        early_hi_ready, early_lo_ready = sem("early_hi_ready"), sem("early_lo_ready")
        raw_in = [sem(f"raw_in{q}") for q in range(Q)]
        diag_ready = sem("diag_ready")
        w_hi_ready, w_lo_ready = sem("w_hi_ready"), sem("w_lo_ready")
        w_used = sem("w_used")
        z_hi_ready, z_lo_ready = sem("z_hi_ready"), sem("z_lo_ready")
        out_act, out_dve = sem("out_act"), sem("out_dve")
        stored = [sem("stored0"), sem("stored1")]
        all_stored = sem("all_stored")

        NCONST = 17

        block = ctx.enter_context(nc.Block())

        def field(engine, s, f, top):
            return engine.value_load(table[0:1, bass.ds(s * FIELDS + f, 1)], min_val=0, max_val=top)

        def slot_loop(engine, body):
            for s in range(1, PEEL):
                body(s, s % 2, s // 2)
            with engine.Fori(PEEL // 2, SURE // 2) as t:
                for par in range(2):
                    body(2 * t + par, par, t)
            with engine.Fori(SURE // 2, SLOTS // 2) as t:
                for par in range(2):
                    active = field(engine, 2 * t + par, F_ACTIVE, 1)
                    with engine.If(active == 1):
                        body(2 * t + par, par, t)

        def last_slot(engine, body):
            but_two = engine.value_load(table[0:1, SLOTS * FIELDS + F_NUMBER:SLOTS * FIELDS + F_NUMBER + 1],
                                  min_val=SURE - 2, max_val=SLOTS - 2)
            odd = field(engine, SLOTS, F_ODD, 1)
            with engine.If(odd == 1):
                body(but_two, 0)
            with engine.Else():
                body(but_two, 1)

        @block.sync
        def _(sp):
            sp.dma_start(params, params_in).then_inc(params_loaded, 16)
            sp.dma_start(control, control_in).then_inc(control_loaded, 16)

            for g in range(NG):
                sp.dma_start(z_group[:, g, :], x_in[g]).then_inc(x_arrived[g % 2], 16)
                if g > 0:
                    sp.wait_ge(x_arrived[(g - 1) % 2], 16 * ((g - 1) // 2 + 1))
                    sp.sem_inc(x_loaded, 1)
            sp.wait_ge(x_arrived[(NG - 1) % 2], 16 * (NG // 2))
            sp.sem_inc(x_loaded, 1)

            def load_strips(g, k):
                if g > 0:
                    sp.wait_ge(conv_done, (g - 1) * NPAIR + k + 1)
                for e in range(2):
                    sp.dma_start(strips[:, k, e, :], strip_source(g * GH + 2 * k + e)).then_inc(strip_in[k][e], 16)

            def load_weights(s, adapter, q):
                if not (isinstance(s, int) and s == 0):
                    sp.wait_ge(w_lo_ready, Q * (s - 1) + q + 1)
                sp.dma_start(raw(s, q).rearrange("p c n -> p (c n)"),
                             w_in[bass.ds(adapter, 1), q].rearrange("o p n -> (o p) n")
                             ).then_inc(raw_in[q], 16)

            sp.wait_ge(zeros_stored, 16)
            for g in range(NG - 1):
                sp.wait_ge(k_stored, 16 * COPIES * (g + 1))
                for k in range(NPAIR):
                    load_strips(g, k)
                if g in EARLY_QUARTERS:
                    if g == EARLY_QUARTERS[0]:
                        sp.wait_ge(least_ready, 1)
                        first_adapter = sp.value_load(least_adapter[0:1, 0:1], min_val=0, max_val=NA - 1)
                    load_weights(0, first_adapter, EARLY_QUARTERS.index(g))
            sp.wait_ge(k_stored, 16 * COPIES * NG)
            for k in range(NPAIR):
                load_strips(NG - 1, k)
            for q in (2, 3):
                load_weights(0, first_adapter, q)
            sp.wait_ge(table_ready, 1)

            def weights_ahead(s):
                first = field(sp, s, F_FIRST, 1)
                adapter = field(sp, s, F_ADAPTER, NA - 1)
                with sp.If(first == 1):
                    for q in range(Q):
                        load_weights(s, adapter, q)
                with sp.Else():
                    for q in range(Q):
                        sp.wait_ge(raw_in[q], 16 * s)
                        sp.sem_inc(raw_in[q], 16)

            def store_slot(s, par):
                b0 = field(sp, s, F_B0, B - 1)
                b1 = field(sp, s, F_B1, B - 1)
                two = field(sp, s, F_TWO, 1)
                sp.wait_ge(out_act, s + 1)
                sp.wait_ge(out_dve, s + 1)
                sp.dma_start(out[bass.ds(b0, 1)].rearrange("o h n -> (o h) n"),
                             o_tile[0:H, par, :]).then_inc(stored[par], 16)
                sp.dma_start(out[bass.ds(b1, 1)].rearrange("o h n -> (o h) n"),
                             o_tile[H:P, par, :], cond=two == 1).then_inc(stored[par], 16)

            def slot(s, par, t):
                weights_ahead(s + 1)
                store_slot(s - 1, 1 - par)

            def finish_last(m, par):
                store_slot(m + 1, par)
                for parity, value in ((par, 16 * (m + 3 - par)), (1 - par, 16 * (m + 1 + par))):
                    sp.wait_ge(stored[parity], value)
                    sp.sem_inc(all_stored, 1)

            weights_ahead(1)
            slot_loop(sp, slot)
            last_slot(sp, finish_last)
            sp.wait_ge(all_stored, 2)

        @block.gpsimd
        def _(pool):
            chain = Chain(pool, pool_step)
            constant = Chain(pool, consts)
            constant.link(nc.gpsimd.memset(quarter[0:N, :], 0.25))
            constant.link(nc.gpsimd.memset(quarter[N:P, :], 0.0))
            constant.link(nc.gpsimd.memset(halfpi[0:N, :], math.pi / 2))
            constant.link(nc.gpsimd.memset(halfpi[N:P, :], 0.0))
            constant.link(nc.gpsimd.memset(sign[0:N, :], 2.0))
            constant.link(nc.gpsimd.memset(lowest[0:N, :], -PI_BELOW - math.pi / 2))
            constant.link(nc.gpsimd.memset(lowest[N:P, :], -PI_BELOW))
            constant.link(nc.gpsimd.memset(highest[0:N, :], PI_BELOW - math.pi / 2))
            constant.link(nc.gpsimd.memset(highest[N:P, :], PI_BELOW))
            constant.link(nc.gpsimd.memset(sign[N:P, :], -2.0))
            exact = dict(allow_small_or_imprecise_dtypes=True)
            constant.link(nc.gpsimd.iota(power[:, 0:S], [[S, S]], base=0, channel_multiplier=0, **exact))
            constant.link(nc.gpsimd.iota(power[:, S:2 * S], [[1, S]], base=0, channel_multiplier=0, **exact))
            constant.link(nc.gpsimd.iota(t_iota, [[P, NB]], base=0, channel_multiplier=1, **exact))
            constant.link(nc.gpsimd.iota(iota_a, [[1, NA]], base=0, channel_multiplier=0, **exact))
            constant.link(nc.gpsimd.iota(iota_pos, [[1, POS]], base=0, channel_multiplier=0, **exact))
            constant.link(nc.gpsimd.iota(values[:, 1:2], [[1, 1]], base=0, channel_multiplier=1, **exact))
            constant.link(nc.gpsimd.memset(ones[:, :], 1.0))
            chain.link(nc.gpsimd.memset(corner, 0.0))
            chain.link(nc.gpsimd.memset(corner[0:1, 0:1], 1.0))
            chain.link(nc.gpsimd.memset(below, 1.0))
            chain.link(nc.gpsimd.affine_select(out=below, in_=below, compare_op=ALU.is_gt, fill=0.0,
                                               base=0, pattern=[[-1, B]], channel_multiplier=1))
            chain.link(nc.gpsimd.memset(ident[:, :], 1.0))
            chain.link(nc.gpsimd.affine_select(out=ident[:, :], in_=ident[:, :], compare_op=ALU.is_equal, fill=0.0,
                                               base=0, pattern=[[-1, P]], channel_multiplier=1))
            constant.link(nc.gpsimd.memset(values[:, 0:1], 1.0))
            pool.wait_ge(dre_ready, 1)
            for h, n in MAG_PARTS:
                nc.gpsimd.tensor_tensor(mag[:, :, h:h + n, :],
                                        dre[:, h:h + n].unsqueeze(1).unsqueeze(3).to_broadcast([P, 2, n, S]),
                                        power.rearrange("p (e s) -> p e s", e=2).unsqueeze(2).to_broadcast([P, 2, n, S]),
                                        ALU.mult).then_inc(e_ready, 1)
            pool.wait_ge(params_loaded, 16)
            chain.link(nc.gpsimd.memset(skip_row[:, :, :], 0.0))
            pool.wait_ge(coef_ready, 2)

            base = chain.n
            PER = 2

            def left_factor(g):
                chain.turn(base + PER * g)
                pool.wait_ge(factor_ready, g + 1)
                if not (isinstance(g, int) and g == 0):
                    pool.wait_ge(k_made, g)
                nc.gpsimd.tensor_copy(skip_row[0:1, :, 0], d_row[0:1, bass.ds(g * GH, GH)]).then_inc(skip_ready, 1)
                chain.link(nc.gpsimd.tensor_tensor(left[:, :, :], factor[:, 0, :, :],
                                                   alpha[:, bass.ds(g * GH, GH)].unsqueeze(2).to_broadcast([P, GH, S]),
                                                   ALU.mult))
                pool.wait_ge(swap_ready, 2 * (g + 1))
                chain.link(nc.gpsimd.tensor_tensor(swapped[:, :, :], swapped[:, :, :],
                                                   beta[:, bass.ds(g * GH, GH)].unsqueeze(2).to_broadcast([P, GH, S]),
                                                   ALU.mult))
                nc.gpsimd.tensor_tensor(left[:, :, :], left[:, :, :], swapped[:, :, :], ALU.add).then_inc(left_ready, 1)

            def add_masked(g, pairs=range(NPAIR)):
                pool.wait_ge(x_loaded, g + 1)
                for k in pairs:
                    n = g * NPAIR + k
                    pool.wait_ge(masked, 2 * (n + 1))
                    nc.gpsimd.tensor_tensor(z_pair[:, bass.ds(n, 1)].rearrange("p o e n -> p (o e n)"),
                                            z_pair[:, bass.ds(n, 1)].rearrange("p o e n -> p (o e n)"),
                                            mid[:, k % 2, :, :].rearrange("p e n -> p (e n)"), ALU.add).then_inc(added, 1)

            left_factor(0)
            left_factor(1)
            with pool.Fori(0, NG - 2) as g:
                left_factor(g + 2)
                add_masked(g)
            add_masked(NG - 2)

            def add_identity(s, quarters=range(Q)):
                for q in quarters:
                    pool.wait_ge(raw_in[q], 16 * (s + 1))
                    for c in range(CQ * q, CQ * (q + 1)):
                        diagonal = raw(s, q)[:, c - CQ * q, c * P:(c + 1) * P]
                        nc.gpsimd.tensor_tensor(diagonal, diagonal,
                                                ident[:, :], ALU.add).then_inc(diag_ready, 1)

            add_identity(0, [0, 1])
            add_masked(NG - 1, [0, 1, 2])
            add_identity(0, [2, 3])

            def slot(s):
                first = field(pool, s, F_FIRST, 1)
                with pool.If(first == 1):
                    add_identity(s)
                with pool.Else():
                    pool.wait_ge(diag_ready, NB * s)
                    pool.sem_inc(diag_ready, NB)

            pool.wait_ge(table_ready, 1)
            with pool.Fori(1, SLOTS) as s:
                slot(s)

        @block.scalar
        def _(act):
            def magnitudes(part):
                act.wait_ge(e_ready, part + 1)
                h, n = MAG_PARTS[part]
                nc.scalar.activation(mag[:, :, h:h + n, :], mag[:, :, h:h + n, :], ACT.Exp).then_inc(mag_ready, 1)

            magnitudes(0)
            act.wait_ge(angles2, 1)
            nc.scalar.activation(sin2, angle2, ACT.Sin).then_inc(sin2_ready, 1)

            def sines(g):
                act.wait_ge(angle_ready, g + 1)
                if not (isinstance(g, int) and g == 0):
                    act.wait_ge(factor_ready, g)
                nc.scalar.activation(sine[:, :, :, :].rearrange("p e h s -> p (e h s)"),
                                     phase[:, :, :, :].rearrange("p e h s -> p (e h s)"),
                                     ACT.Sin, bias=halfpi).then_inc(sine_ready, 1)

            def exchange(g):
                act.wait_ge(factor_ready, g + 1)
                if not (isinstance(g, int) and g == 0):
                    act.wait_ge(left_ready, g)
                nc.scalar.copy(swapped[0:N, :, :], factor[N:P, 0, :, :]).then_inc(swap_ready, 1)
                nc.scalar.copy(swapped[N:P, :, :], factor[0:N, 0, :, :]).then_inc(swap_ready, 1)

            def k_high(g):
                act.wait_ge(k_scaled_ready, g + 1)
                if not (isinstance(g, int) and g == 0):
                    act.wait_ge(k_stored, 16 * COPIES * g)
                nc.scalar.copy(k_tile[:, :, :, 0], k_scaled[:, :, :]).then_inc(k_hi_ready, 1)

            def store_k(g):
                act.wait_ge(k_out, g + 1)
                for q in range(COPIES):
                    act.dma_start(k_rows[bass.ds(g, 1), q].rearrange("o a h b -> (o a) h b"),
                                  k_tile[:, :, :, :].rearrange("a h b two -> a h (b two)").bitcast(f32)
                                  ).then_inc(k_stored, 16)

            def sum_x(g):
                act.wait_ge(x_loaded, g + 1)
                if not (isinstance(g, int) and g == 0):
                    act.wait_ge(x_bound_summed, g)
                for k in range(NPAIR):
                    nc.scalar.activation(magnitude[:, k, :], z_pair[:, bass.ds(g * NPAIR + k, 1)].rearrange("p o e n -> p (o e n)"),
                                         ACT.Abs, accum_out=x_sums[:, k:k + 1]).then_inc(x_sums_ready, 1)

            def x_high(g):
                act.wait_ge(x_scale_ready, g + 1)
                if not (isinstance(g, int) and g < 2):
                    act.wait_ge(conv_done, (g - 1) * NPAIR)
                nc.scalar.activation(x16[:, bass.ds(g % 2, 1), 0, :].rearrange("p o n -> p (o n)"),
                                     z_group[:, bass.ds(g, 1), :].rearrange("p o n -> p (o n)"), ACT.Copy,
                                     scale=x_scale[:, bass.ds(g, 1)]).then_inc(x_hi_ready, 1)

            sines(0)
            act.wait_ge(zeros_ready, 1)
            act.dma_start(k_dram[:, :, 0:P], mid[0:H, 0, :, :].rearrange("h e (q n) -> h (e q) n", n=P)
                          ).then_inc(zeros_stored, 16)
            sum_x(0)
            magnitudes(1)
            exchange(0)
            k_high(0)
            store_k(0)
            x_high(0)
            sines(1)
            exchange(1)
            sum_x(1)
            sines(2)
            k_high(1)
            store_k(1)

            def turn(g):
                if not (isinstance(g, int) and g == 0):
                    sines(g + 2)
                x_high(g + 1)
                exchange(g + 2)
                sum_x(g + 2)
                k_high(g + 2)
                store_k(g + 2)

            turn(0)
            with act.Fori(1, NG - 2) as g:
                turn(g)
            x_high(NG - 1)

            def split_high(s, quarters=range(Q)):
                for q in quarters:
                    act.wait_ge(diag_ready, NB * s + CQ * (q + 1))
                    if not (isinstance(s, int) and s == 0):
                        act.wait_ge(w_used, Q * (s - 1) + q + 1)
                    elif q >= 2:
                        act.wait_ge(w_lo_ready, Q - q)
                    cs = slice(CQ * q, CQ * (q + 1))
                    nc.scalar.copy(w_hi[:, cs, :].rearrange("p c n -> p (c n)"),
                                   raw(s, q).rearrange("p c n -> p (c n)")).then_inc(w_hi_ready, 1)

            def high_parts(b, par, channels, done):
                for j in range(2):
                    nc.scalar.copy(z_hi[:, par, :, j * H + channels.start:j * H + channels.stop],
                                   z_hcb[:, :, channels, bass.ds(b[j], 1)].rearrange("p c h o -> p c (h o)")
                                   ).then_inc(done, 1)

            def gather_high(s, par):
                b = [field(act, s, f, B - 1) for f in (F_B0, F_B1)]
                if not (isinstance(s, int) and s < 2):
                    act.wait_ge(w_used, Q * (s - 1))
                high_parts(b, par, slice(0, H), z_hi_ready)

            def finish(s, par, t):
                act.wait_ge(w_used, Q * (s + 1))
                if not (isinstance(t, int) and t == 0):
                    act.wait_ge(stored[par], 32 * t)
                nc.scalar.copy(o_tile[:, par, 0:HALF], slot_ps[par][0][:, :]).then_inc(out_act, 1)

            def slot(s, par, t):
                gather_high(s, par)
                first = field(act, s, F_FIRST, 1)
                with act.If(first == 1):
                    split_high(s)
                with act.Else():
                    act.wait_ge(w_hi_ready, Q * s)
                    act.sem_inc(w_hi_ready, Q)
                finish(s - 1, 1 - par, t - 1 + par)

            def finish_last(m, par):
                act.wait_ge(w_used, Q * (m + 2))
                act.wait_ge(stored[par], 16 * (m + (1 - par)))
                nc.scalar.copy(o_tile[:, par, 0:HALF], slot_ps[par][0][:, :]).then_inc(out_act, 1)

            split_high(0, [0, 1])
            act.wait_ge(table_ready, 1)
            first_slot = [field(act, 0, f, B - 1) for f in (F_B0, F_B1)]
            act.wait_ge(added, (NG - 1) * NPAIR)
            act.wait_ge(conv_done, (NG - 1) * NPAIR + 2)
            high_parts(first_slot, 0, slice(0, H - GH), early_hi_ready)
            act.wait_ge(added, NG * NPAIR - 1)
            act.wait_ge(added_last, 1)
            high_parts(first_slot, 0, slice(H - GH, H), z_hi_ready)
            split_high(0, [2, 3])
            slot_loop(act, slot)
            last_slot(act, finish_last)

        @block.vector
        def _(dve):
            v = nc.vector
            chain = Chain(dve, dve_step)
            link = chain.link
            steps = Chain(dve, angle_step)
            scale_chain = Chain(dve, scale_step)

            def expm1_parts(x, n):
                k, r, e = kint[:, 0:n], rest[:, 0:n], expm[:, 0:n]
                link(v.tensor_scalar(x, x, -87.0, 88.0, ALU.max, ALU.min))
                link(v.tensor_scalar(k, x, LOG2E, None, ALU.mult))
                link(v.scalar_tensor_tensor(r, k, -LN2_HI, x, ALU.mult, ALU.add))
                link(v.scalar_tensor_tensor(r, k, -LN2_LO, r, ALU.mult, ALU.add))
                link(v.tensor_scalar(e, r, 1.0 / math.factorial(7), None, ALU.mult))
                for d in range(6, 0, -1):
                    link(v.scalar_tensor_tensor(e, e, 1.0 / math.factorial(d), r, ALU.add, ALU.mult))
                link(v.tensor_scalar(scale2[:, 0:n], k, 127.0, float(1 << 23), ALU.add, ALU.mult))

            def reduce_angle(r, k, x, quarters, limits, last, link=link):
                if quarters is None:
                    link(v.tensor_scalar(k, x, INV_2PI, None, ALU.mult))
                else:
                    link(v.tensor_scalar(k, x, INV_2PI, quarters, ALU.mult, ALU.add))
                link(v.scalar_tensor_tensor(x, k, -TWO_PI_HI, x, ALU.mult, ALU.add))
                link(v.scalar_tensor_tensor(r, k, -TWO_PI_LO, x, ALU.mult, ALU.add))
                last(v.tensor_scalar(r, r, *limits, ALU.max, ALU.min))

            v.memset(mid[0:H, 0, :, :], 0.0).then_inc(zeros_ready, 1)
            dve.wait_ge(params_loaded, 16)
            expm1_parts(exponent, 2 * H)
            link(v.scalar_tensor_tensor(expd, expm, 1.0, scale2f, ALU.add, ALU.mult))
            v.scalar_tensor_tensor(dre, ea, -1.0, dt_, ALU.mult, ALU.mult).then_inc(dre_ready, 1)
            link(v.tensor_tensor(dim, a_im, dt_, ALU.mult))
            chain.mark(v.tensor_copy(phase_dim, dim))
            link(v.tensor_scalar(ang2[:, H:2 * H], dim, 0.5, None, ALU.mult))
            reduce_angle(angle2, kint, ang2, None, (-PI_BELOW, PI_BELOW), lambda i: i.then_inc(angles2, 1))
            dve.wait_ge(consts, NCONST + 1)

            def angles(g):
                steps.turn(4 * g)
                if not (isinstance(g, int) and g == 0):
                    dve.wait_ge(sine_ready, g)
                steps.link(v.tensor_tensor(phase[:, :, :, :],
                                     phase_dim[:, bass.ds(g * GH, GH)].unsqueeze(1).unsqueeze(3).to_broadcast([P, 2, GH, S]),
                                     power.rearrange("p (e s) -> p e s", e=2).unsqueeze(2).to_broadcast([P, 2, GH, S]),
                                     ALU.mult))
                flat = [a[:, :, :, :].rearrange("p e h s -> p (e h s)") for a in (phase, turns, phase)]
                reduce_angle(*flat, quarter, (lowest, highest), lambda i: i.then_inc(angle_ready, 1), steps.link)

            def factors(g):
                dve.wait_ge(sine_ready, g + 1)
                dve.wait_ge(mag_ready, 1 if isinstance(g, int) and g < 2 else 2)
                if not (isinstance(g, int) and g == 0):
                    dve.wait_ge(k_made, g)
                v.tensor_tensor(factor[:, :, :, :], sine[:, :, :, :], mag[:, :, bass.ds(g * GH, GH), :],
                                ALU.mult).then_inc(factor_ready, 1)

            def k_scaled_out(g):
                dve.wait_ge(k_made, g + 1)
                if not (isinstance(g, int) and g == 0):
                    dve.wait_ge(k_hi_ready, g)
                v.tensor_tensor(k_scaled[:, :, :], k_ps[0:S, 0:GH * S].rearrange("a (h b) -> a h b", h=GH),
                                k_scale[0:S, bass.ds(g * GH, GH)].unsqueeze(2).to_broadcast([S, GH, S]),
                                ALU.mult).then_inc(k_scaled_ready, 1)

            def k_low(g):
                dve.wait_ge(k_scaled_ready, g + 1)
                dve.wait_ge(k_hi_ready, g + 1)
                v.tensor_tensor(k_tile[:, :, :, 1], k_scaled[:, :, :], k_tile[:, :, :, 0], ALU.subtract
                                ).then_inc(k_out, 1)

            def powers_of_two(bound, exponent_, negated, scale, inverse, link):
                link(v.tensor_scalar(exponent_, bound.bitcast(i32), 2.0 ** -23, -0.25, ALU.mult, ALU.add))
                link(v.tensor_scalar(negated, exponent_, 18.0, -2.0 ** 23, ALU.max, ALU.mult))
                v.tensor_scalar(scale, negated, 1.0, 268.0 * 2.0 ** 23, ALU.mult, ALU.add)
                link(v.tensor_scalar(inverse, negated, -1.0, -14.0 * 2.0 ** 23, ALU.mult, ALU.add))

            def x_scales(g):
                scale_chain.turn(4 * g)
                dve.wait_ge(x_bound_summed, g + 1)
                one = bass.ds(g, 1)
                scale_chain.link(v.tensor_reduce(x_bound, x_bound_ps, AX, ALU.max))
                powers_of_two(x_bound, x_exponent[:, 0:1], x_exponent[:, 1:2], x_scale_i[:, one], x_inverse_i[:, one],
                              scale_chain.link)
                v.tensor_scalar(xk_inverse[:, bass.ds(g * GH, GH)], k_inverse[:, bass.ds(g * GH, GH)],
                                x_inverse[:, one], None, ALU.mult).then_inc(x_scale_ready, 1)

            def x_low(g):
                dve.wait_ge(x_hi_ready, g + 1)
                buffer = x16[:, bass.ds(g % 2, 1), :, :].rearrange("p o e n -> p (o e) n")
                v.scalar_tensor_tensor(buffer[:, 1, :], z_group[:, bass.ds(g, 1), :].rearrange("p o n -> p (o n)"),
                                       x_scale[:, bass.ds(g, 1)], buffer[:, 0, :],
                                       ALU.mult, ALU.subtract).then_inc(x_lo_ready, 1)

            def mask_pair(g, k):
                n = g * NPAIR + k
                dve.wait_ge(conv_done, n + 1)
                if not (isinstance(n, int) and n < 2):
                    dve.wait_ge(added, n - 1)
                dve.wait_ge(x_scale_ready, g + 1)
                for e in range(2):
                    v.scalar_tensor_tensor(mid[:, k % 2, e, :], conv_ps[k][:, e * COL:(e + 1) * COL],
                                           xk_inverse[:, bass.ds(2 * n + e, 1)],
                                           mask[:, :, :].rearrange("p c b -> p (c b)"),
                                           ALU.mult, ALU.mult).then_inc(masked, 1)

            angles(0)

            def halves(t):
                return t.rearrange("p (e h) -> p e h", e=2)

            def both(t):
                return t.unsqueeze(1).to_broadcast([P, 2, H])

            c_ri2, product2, crossed2 = (halves(t) for t in (c_ri, product, crossed))
            chain.mark(v.tensor_scalar(dre_clamped, dre, 1.0, None, ALU.mult))
            chain.mark(v.tensor_tensor(product[:, 0:H], ea, ea, ALU.mult))
            link(v.tensor_tensor(product[:, H:2 * H], a_im, a_im, ALU.mult))
            link(v.tensor_tensor(inverse, product[:, 0:H], product[:, H:2 * H], ALU.add))
            link(v.reciprocal(inverse, inverse))
            chain.mark(v.tensor_tensor(product2, c_ri2, both(ea), ALU.mult))
            link(v.tensor_tensor(crossed2, c_ri2, both(a_im), ALU.mult))
            chain.mark(v.tensor_tensor(c_over_a[:, 0:H], crossed[:, H:2 * H], product[:, 0:H], ALU.subtract))
            link(v.scalar_tensor_tensor(c_over_a[:, H:2 * H], crossed[:, 0:H], -1.0, product[:, H:2 * H],
                                        ALU.mult, ALU.subtract))
            link(v.tensor_tensor(halves(c_over_a), halves(c_over_a), both(inverse), ALU.mult))
            chain.mark(v.tensor_scalar(signed, c_over_a, sign, None, ALU.mult))
            chain.mark(v.tensor_scalar(turned[:, 0:H], c_over_a[:, H:2 * H], -2.0, None, ALU.mult))
            chain.mark(v.tensor_scalar(turned[:, H:2 * H], c_over_a[:, 0:H], -2.0, None, ALU.mult))

            expm1_parts(dre_clamped, H)
            e, sc = expm[:, 0:H], scale2f[:, 0:H]
            link(v.tensor_tensor(e, e, sc, ALU.mult))
            link(v.scalar_tensor_tensor(e, sc, -1.0, e, ALU.add, ALU.add))
            dve.wait_ge(sin2_ready, 1)
            half_sin, full_sin = sin2[:, H:2 * H], sin2[:, 0:H]
            chain.mark(v.scalar_tensor_tensor(e_ri[:, H:2 * H], e, 1.0, full_sin, ALU.add, ALU.mult))
            link(v.scalar_tensor_tensor(product[:, 0:H], half_sin, -2.0, half_sin, ALU.mult, ALU.mult))
            link(v.scalar_tensor_tensor(product[:, 0:H], e, 1.0, product[:, 0:H], ALU.add, ALU.mult))
            link(v.tensor_tensor(e_ri[:, 0:H], e, product[:, 0:H], ALU.add))
            chain.mark(v.tensor_tensor(product, e_ri, signed, ALU.mult))
            link(v.tensor_tensor(crossed, e_ri, turned, ALU.mult))
            v.tensor_tensor(alpha, product[:, 0:H], product[:, H:2 * H], ALU.subtract).then_inc(coef_ready, 1)
            v.tensor_tensor(beta, crossed[:, 0:H], crossed[:, H:2 * H], ALU.add).then_inc(coef_ready, 1)
            factors(0)

            dve.wait_ge(coef_ready, 2)
            bound = c_over_a[:, 0:H]
            chain.mark(v.scalar_tensor_tensor(product, alpha_beta, -1.0, alpha_beta, ALU.mult, ALU.max))
            link(v.scalar_tensor_tensor(crossed[:, 0:H], d_row, -1.0, d_row, ALU.mult, ALU.max))
            link(v.tensor_tensor(product[:, 0:H], product[:, 0:H], product[:, H:2 * H], ALU.add))
            v.scalar_tensor_tensor(bound, crossed[:, 0:H], 1.0 / P, product[:, 0:H], ALU.mult, ALU.add
                                   ).then_inc(bound_ready, 1)
            dve.wait_ge(k_bound_summed, 1)
            powers_of_two(k_bound_ps, kint[:, 0:H], kint[:, H:2 * H], k_scale_i, k_inverse_i, link)
            x_scales(0)
            k_scaled_out(0)
            k_low(0)
            angles(1)
            x_low(0)
            factors(1)
            dve.wait_ge(control_loaded, 16)
            link(v.tensor_copy(lens, lens_i))
            link(v.tensor_tensor(mask[:, :, :], lens.unsqueeze(1).to_broadcast([P, NB, B]),
                                 t_iota.unsqueeze(2).to_broadcast([P, NB, B]), ALU.is_gt))

            angles(2)

            link(v.tensor_scalar(wrap, ids_i, 0.0, float(NA), ALU.is_lt, ALU.mult))
            link(v.tensor_tensor(ids, ids_i, wrap, ALU.add))
            link(v.tensor_scalar(ids, ids, 0.0, NA - 1.0, ALU.max, ALU.min))
            v.tensor_reduce(least_adapter, ids[0:1, 0:B], AX, ALU.min).then_inc(least_ready, 1)
            link(v.tensor_scalar(same, ids[:, 0:B], own, None, ALU.is_equal))
            link(v.tensor_tensor(same, same, below, ALU.mult))
            link(v.reduce_sum(rank, same, AX))
            is_a3 = is_a.rearrange("p (a b) -> p a b", a=NA)
            link(v.tensor_tensor(is_a3, ids[:, 0:B].unsqueeze(1).to_broadcast([B, NA, B]),
                                 iota_a.unsqueeze(2).to_broadcast([B, NA, B]), ALU.is_equal))
            link(v.reduce_sum(count, is_a3, AX))
            link(v.tensor_scalar(pairs_i, count, 0.5, 0.25, ALU.mult, ALU.add))
            link(v.tensor_scalar(less, iota_a, own, None, ALU.is_lt))
            link(v.tensor_tensor(less, less, pairs_i, ALU.mult))
            link(v.reduce_sum(before, less, AX))
            link(v.scalar_tensor_tensor(pos, before, 2.0, rank, ALU.mult, ALU.add))
            link(v.tensor_scalar(match, iota_pos, pos, None, ALU.is_equal))
            v.tensor_copy(values[:, 2:3], own).then_inc(slots_placed, 1)

            k_scaled_out(1)
            k_low(1)
            x_scales(1)
            dve.wait_ge(zeros_stored, 16)

            def turn(g):
                if not (isinstance(g, int) and g == 0):
                    angles(g + 2)
                    mask_pair(g - 1, NPAIR - 1)
                factors(g + 2)
                mask_pair(g, 0)
                x_low(g + 1)
                mask_pair(g, 1)
                mask_pair(g, 2)
                k_scaled_out(g + 2)
                x_scales(g + 2)
                k_low(g + 2)

            turn(0)
            with dve.Fori(1, NG - 2) as g:
                turn(g)
            dve.wait_ge(table_rows, 1)
            link(v.tensor_copy(row[0:1, 0:3, :], table_ps[0:1, 0:3 * POS].rearrange("p (f n) -> p f n", f=3)))
            there, batch, adapter = (row[0:1, f, :].rearrange("p (s j) -> p j s", j=2) for f in range(3))
            ns = SLOTS + 1
            out_t = table[0:1, :].rearrange("p (s f) -> p f s", f=FIELDS)
            change, fill = row[0:1, 3, 0:ns], row[0:1, 4, 0:ns]
            number, odd = row[0:1, 5, 0:1], row[0:1, 6, 0:1]
            link(v.memset(table[0:1, :], 0))
            link(v.memset(change, 1.0))
            link(v.tensor_tensor(change[:, 1:ns], adapter[:, 0, 1:ns], adapter[:, 0, 0:ns - 1], ALU.not_equal))
            link(v.tensor_scalar(fill, there[:, 1, :], -1.0, 1.0, ALU.mult, ALU.add))
            link(v.tensor_tensor(fill, fill, batch[:, 0, :], ALU.mult))
            link(v.reduce_sum(number, there[:, 0, :], AX))
            link(v.tensor_copy(out_t[:, F_B0, :], batch[:, 0, :]))
            link(v.tensor_tensor(out_t[:, F_B1, :], batch[:, 1, :], fill, ALU.add))
            link(v.tensor_tensor(out_t[:, F_FIRST, :], change, there[:, 0, :], ALU.mult))
            link(v.tensor_copy(out_t[:, F_ADAPTER, :], adapter[:, 0, :]))
            link(v.tensor_copy(out_t[:, F_TWO, :], there[:, 1, :]))
            link(v.tensor_copy(out_t[:, F_ACTIVE, :], there[:, 0, :]))
            link(v.tensor_scalar(out_t[:, F_NUMBER, ns - 1:ns], number, -2.0, None, ALU.add))
            link(v.tensor_scalar(out_t[:, F_ODD, ns - 1:ns], number, 0.5, -0.25, ALU.mult, ALU.add))
            link(v.tensor_copy(odd, out_t[:, F_ODD, ns - 1:ns]))
            link(v.scalar_tensor_tensor(out_t[:, F_ODD, ns - 1:ns], odd, -2.0, number, ALU.mult, ALU.add))
            v.memset(table[0:1, 6:7], 0).then_inc(table_ready, 1)

            mask_pair(NG - 3, NPAIR - 1)
            x_low(NG - 1)
            mask_pair(NG - 2, 0)
            mask_pair(NG - 2, 1)

            mask_pair(NG - 2, 2)
            mask_pair(NG - 2, 3)

            def split_low(s, q):
                dve.wait_ge(w_hi_ready, Q * s + q + 1)
                cs = slice(CQ * q, CQ * (q + 1))
                v.tensor_tensor(w_lo[:, cs, :], raw(s, q), w_hi[:, cs, :].bitcast(f32),
                                ALU.subtract).then_inc(w_lo_ready, 1)

            def low_parts(b, par, channels, done):
                for j in range(2):
                    v.tensor_tensor(z_lo[:, par, :, j * H + channels.start:j * H + channels.stop],
                                    z_hcb[:, :, channels, bass.ds(b[j], 1)].rearrange("p c h o -> p c (h o)"),
                                    z_hi[:, par, :, j * H + channels.start:j * H + channels.stop].bitcast(f32),
                                    ALU.subtract).then_inc(done, 1)

            def gather_low(s, par):
                b = [field(dve, s, f, B - 1) for f in (F_B0, F_B1)]
                dve.wait_ge(z_hi_ready, 2 * (s + 1))
                low_parts(b, par, slice(0, H), z_lo_ready)

            def finish(s, par, t):
                dve.wait_ge(w_used, Q * (s + 1))
                if not (isinstance(t, int) and t == 0):
                    dve.wait_ge(stored[par], 32 * t)
                v.tensor_copy(o_tile[:, par, HALF:L], slot_ps[par][1][:, :]).then_inc(out_dve, 1)

            def slot(s, par, t):
                gather_low(s, par)
                first = field(dve, s, F_FIRST, 1)
                with dve.If(first == 1):
                    for q in range(Q):
                        split_low(s, q)
                with dve.Else():
                    dve.wait_ge(w_lo_ready, Q * s)
                    dve.sem_inc(w_lo_ready, Q)
                finish(s - 1, 1 - par, t - 1 + par)

            def finish_last(m, par):
                dve.wait_ge(w_used, Q * (m + 2))
                dve.wait_ge(stored[par], 16 * (m + (1 - par)))
                v.tensor_copy(o_tile[:, par, HALF:L], slot_ps[par][1][:, :]).then_inc(out_dve, 1)

            split_low(0, 0)
            mask_pair(NG - 1, 0)
            split_low(0, 1)
            mask_pair(NG - 1, 1)
            first_slot = [field(dve, 0, f, B - 1) for f in (F_B0, F_B1)]
            dve.wait_ge(early_hi_ready, 2)
            low_parts(first_slot, 0, slice(0, H - GH), early_lo_ready)
            mask_pair(NG - 1, 2)
            mask_pair(NG - 1, NPAIR - 1)
            dve.wait_ge(masked, 2 * NG * NPAIR)
            dve.wait_ge(x_loaded, NG)
            last_pair = z_pair[:, H // 2 - 1, :, :].rearrange("p e n -> p (e n)")
            v.tensor_tensor(last_pair, last_pair, mid[:, (NPAIR - 1) % 2, :, :].rearrange("p e n -> p (e n)"),
                            ALU.add).then_inc(added_last, 1)
            dve.wait_ge(z_hi_ready, 2)
            low_parts(first_slot, 0, slice(H - GH, H), z_lo_ready)
            for q in (2, 3):
                split_low(0, q)
            slot_loop(dve, slot)
            last_slot(dve, finish_last)

        @block.tensor
        def _(pe):
            mm = nc.tensor.matmul

            def k_rows_made(g):
                pe.wait_ge(left_ready, g + 1)
                pe.wait_ge(skip_ready, g + 1)
                if not (isinstance(g, int) and g == 0):
                    pe.wait_ge(k_scaled_ready, g)
                mm(k_ps[0:S, 0:GH * S], corner, skip_row[:, :, :].rearrange("p h b -> p (h b)"),
                   start=True, stop=False)
                for i in range(GH):
                    last = mm(k_ps[0:S, i * S:(i + 1) * S], left[:, i, :], factor[:, 1, i, :], start=False,
                              stop=(i == GH - 1))
                last.then_inc(k_made, 1)

            def convolve(g, k):
                if k == 0:
                    pe.wait_ge(x_lo_ready, g + 1)
                if not (isinstance(g, int) and g == 0):
                    pe.wait_ge(masked, 2 * ((g - 1) * NPAIR + k + 1))
                for e in range(2):
                    pe.wait_ge(strip_in[k][e], 16 * (g + 1))
                    col = (2 * k + e) * COL
                    for d in range(NB):
                        for k_part, x_part in ((0, 0), (0, 1), (1, 0)):
                            last = mm(conv_ps[k][:, e * COL + d * B:(e + 1) * COL], strips16[:, k, e, k_part, d, :],
                                      x16[:, bass.ds(g % 2, 1), x_part, col:col + (NB - d) * B].rearrange("p o n -> p (o n)"),
                                      start=(d == 0 and k_part == x_part), stop=(d == NB - 1 and k_part == 1))
                last.then_inc(conv_done, 1)

            def sum_x_bound(g):
                pe.wait_ge(x_sums_ready, NPAIR * (g + 1))
                if not (isinstance(g, int) and g == 0):
                    pe.wait_ge(x_scale_ready, g)
                mm(x_bound_ps, ones[:, :], x_sums, start=True, stop=True).then_inc(x_bound_summed, 1)

            pe.wait_ge(consts, NCONST + 1)
            sum_x_bound(0)
            pe.wait_ge(bound_ready, 1)
            mm(k_bound_ps, ones[:, :], c_over_a[:, 0:H], start=True, stop=True).then_inc(k_bound_summed, 1)
            k_rows_made(0)

            def turn(g):
                convolve(g, 0)
                if isinstance(g, int) and g == 0:
                    k_rows_made(1)
                    sum_x_bound(1)
                convolve(g, 1)
                convolve(g, 2)
                k_rows_made(g + 2)
                sum_x_bound(g + 2)
                convolve(g, 3)

            turn(0)
            with pe.Fori(1, NG - 2) as g:
                turn(g)
            pe.wait_ge(slots_placed, 1)
            for f in range(3):
                last = mm(table_ps[0:1, f * POS:(f + 1) * POS], values[:, f:f + 1], match, start=True, stop=True)
            last.then_inc(table_rows, 1)
            for g in (NG - 2, NG - 1):
                for k in range(NPAIR):
                    convolve(g, k)

            def slot(s, par, t):
                pe.wait_ge(z_lo_ready, 2 * (s + 1))
                if not (isinstance(s, int) and s < 2):
                    pe.wait_ge(out_act, s - 1)
                    pe.wait_ge(out_dve, s - 1)
                for q in range(Q):
                    pe.wait_ge(w_lo_ready, Q * s + q + 1)
                    for c in range(CQ * q, CQ * (q + 1)):
                        for left_, right in ((z_hi, w_hi), (z_hi, w_lo), (z_lo, w_hi)):
                            for half in range(2):
                                last = mm(slot_ps[par][half][:, :], left_[:, par, c, :],
                                          right[:, c, half * HALF:(half + 1) * HALF],
                                          start=(c == 0 and left_ is z_hi and right is w_hi),
                                          stop=(c == NB - 1 and left_ is z_lo))
                    last.then_inc(w_used, 1)

            pe.wait_ge(masked, 2 * NG * NPAIR)
            pe.wait_ge(early_lo_ready, 2)
            slot(0, 0, 0)
            slot_loop(pe, slot)


def kernel(**inputs):
    import numpy as np
    import concourse.bacc as bacc
    from concourse import mybir as mb
    from concourse.bass_utils import run_bass_kernel_spmd

    x = np.asarray(inputs["x"])
    B, H, L = x.shape
    P, GH, Q = 128, 8, 4
    NB = L // P
    ids, lens = np.asarray(inputs["itok_B_3_7"]), np.asarray(inputs["itok_B_8_3872"])
    log_dt, log_a, a_imag, c, d = (np.asarray(inputs["L0_cond_" + name])
                                   for name in ("log_dt", "log_A_real", "A_imag", "C", "D"))
    w = np.asarray(inputs["L1_cond_weight"])
    NA = w.shape[0]
    arrays = {
        "x": x.reshape(B, H // GH, GH, NB, P).transpose(1, 4, 2, 3, 0).reshape(H // GH, P, GH * NB * B),
        "control": np.concatenate([np.tile(lens, (P, 1)), np.tile(ids, (P, 1)), np.tile(ids, P // B)[:, None]], 1),
        "params": np.concatenate([np.tile(log_dt, (P, 1)), *(np.tile(m.T, (2, 1)) for m in (log_a, a_imag, c[..., 0], c[..., 1])),
                                  np.tile(d, (P, 1))], 1),
        "w": w.reshape(NA, L, Q, NB // Q, P).transpose(0, 2, 4, 3, 1).reshape(NA, Q, P, NB // Q * L),
    }
    arrays = {k: np.ascontiguousarray(v) for k, v in arrays.items()}
    nc = bacc.Bacc("TRN2", target_bir_lowering=False, num_devices=1)
    args = [nc.dram_tensor(f"in_{k}", v.shape, mb.dt.from_np(v.dtype), kind="ExternalInput").ap() for k, v in arrays.items()]
    out = nc.dram_tensor("out", (B, H, L), mb.dt.float32, kind="ExternalOutput").ap()
    ssm_conv_then_adapter_kernel(nc, *args, out)
    return run_bass_kernel_spmd(nc, [{f"in_{k}": v for k, v in arrays.items()}], core_ids=[0]).results[0]["out"]
```
